# Optimizing a Trainium2 kernel written in Bass

```python
import numpy as np
import jax
import jax.numpy as jnp

def _softmax(x, axis=-1):
    return jax.nn.softmax(x, axis=axis)

def _gelu(x):
    return jax.nn.gelu(x, approximate=True)

def _silu(x):
    return jax.nn.silu(x)

def _sigmoid(x):
    return jax.nn.sigmoid(x)

def _layernorm(x, axis=-1, eps=1e-05):
    m = jnp.mean(x, axis=axis, keepdims=True)
    v = jnp.var(x, axis=axis, keepdims=True)
    return (x - m) / jnp.sqrt(v + eps)

def _scatter_add(tgt, idx, src, axis=0):
    return tgt.at[idx].add(src)

def _segment_sum(src, seg, n):
    return jax.ops.segment_sum(src, seg, n)
kernel_name = 'mk_gnn_preln_d2_gnn_r8_390278'

def setup_inputs(seed: int=0):
    np.random.seed(seed)
    _w = jnp.asarray

    def _rec_inputs():
        import jax
        import jax.numpy as jnp
        _gk = jax.random.key(seed)
        x = -8.776e-05 + 1 * jax.random.normal(jax.random.fold_in(_gk, 1), (12500, 64), jnp.float32)
        src = jax.random.randint(jax.random.fold_in(_gk, 2), (400000,), 0, 12500, jnp.int32)
        dst = jax.random.randint(jax.random.fold_in(_gk, 3), (400000,), 0, 12500, jnp.int32)
        _o = jnp.argsort(dst, stable=True)
        src = src[_o]
        dst = dst[_o]
        edge_attr_32 = 0.000167468 + 1.0002 * jax.random.normal(jax.random.fold_in(_gk, 11), (400000, 32), jnp.float32)
        return (x, src, dst, edge_attr_32)
    x, src, dst, edge_attr_32 = _rec_inputs()

    def _L0_gnn_setup():
        import jax, jax.numpy as jnp
        import numpy as np
        EPS = 1e-05

        def _layernorm(x, g, b):
            mu = jnp.mean(x, axis=-1, keepdims=True)
            var = jnp.mean((x - mu) ** 2, axis=-1, keepdims=True)
            return (x - mu) * jax.lax.rsqrt(var + EPS) * g + b
        N, E, IN, ED, OUT = (10000, 160000, 64, 32, 64)
        key = jax.random.key(seed)
        ks = jax.random.split(key, 12)

        def lin(k, fan_in, shape):
            bound = 1.0 / np.sqrt(fan_in)
            return jax.random.uniform(k, shape, jnp.float32, -bound, bound)
        return {'node_features': jax.random.normal(ks[0], (N, IN), jnp.float32), 'edge_index': jax.random.randint(ks[1], (2, E), 0, N, jnp.int64), 'edge_features': jax.random.normal(ks[2], (E, ED), jnp.float32), 'W1': lin(ks[3], IN + ED, (IN + ED, OUT)), 'b1': lin(ks[4], IN + ED, (OUT,)), 'g1': jnp.ones((OUT,), jnp.float32), 'be1': jnp.zeros((OUT,), jnp.float32), 'W2': lin(ks[5], OUT, (OUT, OUT)), 'b2': lin(ks[6], OUT, (OUT,)), 'Wu': lin(ks[7], OUT + IN, (OUT + IN, OUT)), 'bu': lin(ks[8], OUT + IN, (OUT,)), 'gn': jnp.ones((OUT,), jnp.float32), 'bn': jnp.zeros((OUT,), jnp.float32)}
    _L0_gnn_all = _L0_gnn_setup()
    _L0_gnn_in = {k: v for k, v in _L0_gnn_all.items() if k in ('W1', 'b1', 'g1', 'be1', 'W2', 'b2', 'Wu', 'bu', 'gn', 'bn')}
    del _L0_gnn_all

    def _L1_gnn_setup():
        import jax, jax.numpy as jnp
        import numpy as np
        EPS = 0.0
        key = jax.random.key(seed)
        ks = jax.random.split(key, 5)
        N, E, D_IN, D_H, D_OUT = (6250, 100000, 64, 256, 64)
        x = jax.random.normal(ks[0], (N, D_IN), dtype=jnp.float32)
        edge_index = jax.random.randint(ks[1], (2, E), 0, N, dtype=jnp.int64)
        W1 = jax.random.normal(ks[2], (D_IN, D_H), dtype=jnp.float32) * (1.0 / np.sqrt(D_IN))
        b1 = jnp.zeros((D_H,), dtype=jnp.float32)
        W2 = jax.random.normal(ks[3], (D_H, D_OUT), dtype=jnp.float32) * (1.0 / np.sqrt(D_H))
        b2 = jnp.zeros((D_OUT,), dtype=jnp.float32)
        return {'x': x, 'edge_index': edge_index, 'W1': W1, 'b1': b1, 'W2': W2, 'b2': b2}
    _L1_gnn_all = _L1_gnn_setup()
    _L1_gnn_in = {k: v for k, v in _L1_gnn_all.items() if k in ('W1', 'b1', 'W2', 'b2')}
    del _L1_gnn_all
    return {'x': x, 'src': src, 'dst': dst, 'edge_attr_32': edge_attr_32, 'L0_gnn_W1': _L0_gnn_in['W1'], 'L0_gnn_b1': _L0_gnn_in['b1'], 'L0_gnn_g1': _L0_gnn_in['g1'], 'L0_gnn_be1': _L0_gnn_in['be1'], 'L0_gnn_W2': _L0_gnn_in['W2'], 'L0_gnn_b2': _L0_gnn_in['b2'], 'L0_gnn_Wu': _L0_gnn_in['Wu'], 'L0_gnn_bu': _L0_gnn_in['bu'], 'L0_gnn_gn': _L0_gnn_in['gn'], 'L0_gnn_bn': _L0_gnn_in['bn'], 'L1_gnn_W1': _L1_gnn_in['W1'], 'L1_gnn_b1': _L1_gnn_in['b1'], 'L1_gnn_W2': _L1_gnn_in['W2'], 'L1_gnn_b2': _L1_gnn_in['b2']}

def reference(x, src, dst, edge_attr_32, L0_gnn_W1, L0_gnn_b1, L0_gnn_g1, L0_gnn_be1, L0_gnn_W2, L0_gnn_b2, L0_gnn_Wu, L0_gnn_bu, L0_gnn_gn, L0_gnn_bn, L1_gnn_W1, L1_gnn_b1, L1_gnn_W2, L1_gnn_b2):
    import jax
    import jax.numpy as jnp

    def _L0_gnn_ref(node_features, edge_index, edge_features, W1, b1, g1, be1, W2, b2, Wu, bu, gn, bn):
        import jax, jax.numpy as jnp
        import numpy as np
        EPS = 1e-05

        def _layernorm(x, g, b):
            mu = jnp.mean(x, axis=-1, keepdims=True)
            var = jnp.mean((x - mu) ** 2, axis=-1, keepdims=True)
            return (x - mu) * jax.lax.rsqrt(var + EPS) * g + b
        src_idx, tgt_idx = (edge_index[0], edge_index[1])
        N = node_features.shape[0]
        src_feats = node_features[src_idx]
        h = jnp.concatenate([src_feats, edge_features], axis=-1)
        h = jax.nn.silu(_layernorm(h @ W1 + b1, g1, be1))
        messages = jax.nn.silu(h @ W2 + b2)
        agg = jax.ops.segment_sum(messages, tgt_idx, num_segments=N)
        combined = jnp.concatenate([agg, node_features], axis=-1)
        updated = jax.nn.silu(combined @ Wu + bu)
        return _layernorm(updated, gn, bn)

    def _L1_gnn_ref(x, edge_index, W1, b1, W2, b2):
        import jax, jax.numpy as jnp
        import numpy as np
        EPS = 0.0
        src, dst = (edge_index[0], edge_index[1])
        msgs = x[src]
        agg = jax.ops.segment_sum(msgs, dst, num_segments=x.shape[0])
        h = (1.0 + EPS) * x + agg
        h = jnp.maximum(h @ W1 + b1, 0.0)
        return h @ W2 + b2
    edge_index = jnp.stack([src, dst])
    h = jnp.maximum(_layernorm(x, axis=-1), 0.0)
    x = x + _L0_gnn_ref(h, edge_index, edge_attr_32, L0_gnn_W1, L0_gnn_b1, L0_gnn_g1, L0_gnn_be1, L0_gnn_W2, L0_gnn_b2, L0_gnn_Wu, L0_gnn_bu, L0_gnn_gn, L0_gnn_bn)
    h = jnp.maximum(_layernorm(x, axis=-1), 0.0)
    x = x + _L1_gnn_ref(h, edge_index, L1_gnn_W1, L1_gnn_b1, L1_gnn_W2, L1_gnn_b2)
    return x

_drawn_inputs = setup_inputs


def setup_inputs(seed=0):
    import zlib

    import numpy as np

    out = dict(_drawn_inputs(seed))
    spreads = {'L0_gnn_g1': (1.0, 0.2),
     'L0_gnn_be1': (0.0, 0.1),
     'L0_gnn_gn': (1.0, 0.2),
     'L0_gnn_bn': (0.0, 0.1),
     'L1_gnn_b1': (0.0, 0.8),
     'L1_gnn_b2': (0.0, 0.8)}
    factors = {'L0_gnn_bu': 2.668}
    for name, (base, spread) in spreads.items():
        noise = np.random.default_rng([zlib.crc32(name.encode()), seed]).standard_normal(out[name].shape)
        drawn = base * np.exp(spread * noise) if base else spread * noise
        out[name] = jnp.asarray(drawn.astype(out[name].dtype))
    for name, factor in factors.items():
        out[name] = (out[name] * factor).astype(out[name].dtype)
    return out
```

```python
import concourse.bass as bass
from concourse import mybir
from contextlib import ExitStack


def build_gnn(nc, x, src, dst, edge_t, W1, b1, g1, be1, W2, b2, Wu, bu, gn, bn, M1, c1, M2, c2, out):
    f32, i32 = mybir.dt.float32, mybir.dt.int32
    ALU = mybir.AluOpType
    ACT = mybir.ActivationFunctionType
    X = mybir.AxisListType.X
    EPS = 1e-5

    N, F = x.shape
    ED = edge_t.shape[1]
    BLOCKS, BC = src.shape[1], src.shape[2]
    EB = 128 * BC
    UN = 5
    ROUNDS = BLOCKS // UN
    WIN = 64
    WINDOWS = -(-N // WIN)
    H = M1.shape[1]
    HS = H // 128
    TP = max(t for t in range(1, 129) if N % t == 0)
    T = N // TP
    Q = 4
    CH = 20 if T % 20 == 0 else Q
    CHUNKS = T // CH
    BQ = CH // Q
    PAIRS = -(-BC // 2)
    assert BLOCKS % UN == 0 and T % CH == 0 and CH % Q == 0 and F == 64 and ED == 32 and TP * Q <= 512

    ctx = ExitStack()
    with ctx:
        def sb(name, shape, dt=f32):
            return ctx.enter_context(nc.sbuf_tensor(name, shape, dt))

        def sem(name):
            return ctx.enter_context(nc.semaphore(name))

        ptab = nc.dram_tensor("layer0_rows", (N, F), f32, kind="Internal").ap()
        htab = nc.dram_tensor("layer1_rows", (N, F), f32, kind="Internal").ap()

        xs = sb("xs", [TP, T, F])
        cT = sb("cT", [128, N + WIN + 64])
        src_all = sb("src_all", [128, BLOCKS, BC], i32)
        dst_all = sb("dst_all", [128, BLOCKS, BC], i32)
        rel_all = sb("rel_all", [128, BLOCKS, BC])
        base_row = sb("base_row", [1, BLOCKS])
        base_int = sb("base_int", [1, BLOCKS], i32)
        flag = sb("flag", [1, 1], i32)
        worst = sb("worst", [128, 3])
        worst_row = sb("worst_row", [1, 1])

        w1n = sb("w1n", [128, F])
        w1e = sb("w1e", [ED, F])
        b1r = sb("b1r", [1, F])
        wmean = sb("wmean", [128, 3])
        w2d = sb("w2d", [128, 128])
        wu = sb("wu", [128, F])
        m1 = sb("m1", [F, H])
        m2 = sb("m2", [128, HS, F])
        gcol = sb("gcol", [128, 2])
        c1col = sb("c1col", [128, HS])
        rows = sb("rows", [1, 5, F])
        b2rep = sb("b2rep", [1, BC, F])
        gb = sb("gb", [128, 2, F])
        ones = sb("ones", [1, 128])
        iot = sb("iot", [128, 128], i32)
        ident = sb("ident", [128, 128])
        wint = sb("wint", [128, BC, WIN], i32)
        winf = sb("winf", [128, BC, WIN])
        wbase = sb("wbase", [128, 1])

        xc = sb("xc", [TP, CH, F])
        sqc = sb("sqc", [TP, CH, F])
        hpad = sb("hpad", [TP, CH, 2 * F])
        stat = sb("stat", [TP, 4, CH])
        prow = sb("prow", [TP, CH, F])
        hid = sb("hid", [128, HS, Q * TP])
        cols = sb("cols", [128, 2, Q * TP])

        idx = sb("idx", [128, UN, BC], i32)
        ea = sb("ea", [ED, UN, EB])
        gat = sb("gat", [128, UN, 2 * PAIRS, F])
        oh = sb("oh", [128, UN, BC, WIN])
        sq = sb("sq", [128, 2, BC, F])
        st = sb("st", [128, 2, 2, BC])
        hT = sb("hT", [128, UN, PAIRS * 128])
        msg = sb("msg", [128, UN, BC, F])
        reln = sb("reln", [128, BC])

        zp = [ctx.enter_context(nc.psum_tensor(f"zp{i}", [128, 512], f32)) for i in range(2)]
        tp = [ctx.enter_context(nc.psum_tensor(f"tp{i}", [128, 512], f32)) for i in range(2)]
        mp = [ctx.enter_context(nc.psum_tensor(f"mp{i}", [128, 512], f32)) for i in range(2)]
        ag = [ctx.enter_context(nc.psum_tensor(f"ag{i}", [128, 512], f32)) for i in range(2)]

        x_t = x.rearrange("(t p) f -> p t f", p=TP)
        out_t = out.rearrange("(t p) f -> p t f", p=TP)
        ptab_t = ptab.rearrange("(t p) f -> p t f", p=TP)
        htab_t = htab.rearrange("(t p) f -> p t f", p=TP)

        def bcast(a, n):
            return a.unsqueeze(2).broadcast_to([a.shape[0], a.shape[1], n])

        def per_tile(a, n):
            return a.unsqueeze(1).broadcast_to([a.shape[0], n, a.shape[1]])

        NORM = 15
        def wait(eng, semaphore, value):
            if not isinstance(value, int) or value > 0:
                eng.wait_ge(semaphore, value)

        def repeated(eng, count, body):
            body(0)
            with eng.Fori(1, count) as g:
                body(g)

        turns = {}

        def wait_alone(eng, name):
            if name not in turns:
                turns[name] = sem(f"turns_of_{name}")
            eng.sem_inc(turns[name], 1)

        RSTD = 12

        def rstd(v, total, y, t, step, base):
            yi, ti = y.bitcast(i32), t.bitcast(i32)
            v.tensor_scalar(total, total, 1.0 / F, EPS, ALU.mult, ALU.add).then_inc(step, 1)
            v.wait_ge(step, base + 1)
            v.tensor_scalar(ti, total.bitcast(i32), 1, None, ALU.logical_shift_right).then_inc(step, 1)
            v.wait_ge(step, base + 2)
            v.tensor_scalar(yi, ti, -1.0, float(0x5F3759DF), ALU.mult, ALU.add).then_inc(step, 1)
            for k in range(3):
                v.wait_ge(step, base + 3 + 3 * k)
                v.scalar_tensor_tensor(t, y, -0.5, y, ALU.mult, ALU.mult).then_inc(step, 1)
                v.wait_ge(step, base + 4 + 3 * k)
                v.tensor_tensor(t, t, total, ALU.mult).then_inc(step, 1)
                v.wait_ge(step, base + 5 + 3 * k)
                v.scalar_tensor_tensor(y, t, 1.5, y, ALU.add, ALU.mult).then_inc(step, 1)
            v.wait_ge(step, base + 12)

        s_w = sem("weights_loaded")
        s_i = sem("edges_loaded")
        s_x = sem("x_loaded")
        s_iota = sem("iota_ready")
        s_const = sem("constants_ready")
        s_dstep = sem("setup_vector_steps")
        s_bp = sem("bases_broadcast")
        s_wt = sem("worst_transposed")
        s_cen = sem("centred")
        s_sqd = sem("squared")
        s_norm = sem("normalised")
        s_pad = sem("pad_ready")
        s_padfree = sem("pad_free")
        s_tr = sem("transposed")
        s_cp = sem("columns_copied")
        s_cT = sem("columns_in_place")
        s_pr = sem("rows_multiplied")
        s_prc = sem("rows_copied")
        s_ps = sem("rows_stored")
        WL = 16 * 19

        with nc.Block() as block:
            @block.sync
            def _(sp):
                sp.dma_start(xs[:, :, :], x_t).then_inc(s_x, 16)
                sp.dma_start(dst_all[:, :, :], dst).then_inc(s_i, 16)
                sp.dma_start(src_all[:, :, :], src).then_inc(s_i, 16)
                sp.dma_start(w1n[F:2 * F, :], W1[0:F, :]).then_inc(s_w, 16)
                sp.dma_start(w1e[:, :], W1[F:F + ED, :]).then_inc(s_w, 16)
                sp.dma_start(b1r[:, :], b1.unsqueeze(0)).then_inc(s_w, 16)
                sp.dma_start(wu[:, :], Wu).then_inc(s_w, 16)
                sp.dma_start(m1[:, :], M1).then_inc(s_w, 16)
                sp.dma_start(m2[:, :, :], M2.rearrange("(h p) f -> p h f", p=128)).then_inc(s_w, 16)
                for h in range(HS):
                    sp.dma_start(c1col[:, h:h + 1], c1[h * 128:(h + 1) * 128].unsqueeze(1)).then_inc(s_w, 16)
                for k in range(2):
                    sp.dma_start(gcol[k * F:(k + 1) * F, 0:1], g1.unsqueeze(1)).then_inc(s_w, 16)
                    sp.dma_start(gcol[k * F:(k + 1) * F, 1:2], be1.unsqueeze(1)).then_inc(s_w, 16)
                for k, row in enumerate((b2, bu, gn, bn, c2)):
                    sp.dma_start(rows[:, k, :], row.unsqueeze(0)).then_inc(s_w, 16)
                sp.wait_ge(s_const, 1)
                for k in range(2):
                    sp.dma_start(w2d[k * F:(k + 1) * F, k * F:(k + 1) * F], W2).then_inc(s_w, 16)
                def chunk(g):
                    wait(sp, s_prc, BQ * g + BQ)
                    sp.dma_start(ptab_t[:, bass.ds(g * CH, CH), :], prow[:, :, :]).then_inc(s_ps, 16)
                repeated(sp, CHUNKS, chunk)
                sp.wait_ge(s_ps, 16 * CHUNKS)
                sp.wait_ge(s_i, 32)

            @block.gpsimd
            def _(pool):
                pool.iota(iot[:, :], [[1, 128]], base=0, channel_multiplier=-1).then_inc(s_iota, 1)
                pool.iota(wint[:, :, :], [[0, BC], [1, WIN]], base=0, channel_multiplier=0).then_inc(s_iota, 1)
                def chunk(g):
                    for q in range(BQ):
                        wait(pool, s_cp, BQ * g + q + 1)
                        pool.tensor_copy(cT[:, bass.ds(g * (CH * TP) + q * Q * TP, Q * TP)],
                                         cols[:, q % 2, :]).then_inc(s_cT, 1)
                repeated(pool, CHUNKS, chunk)

            @block.vector
            def _(v):
                v.memset(w2d[:, :], 0.0).then_inc(s_const, 1)
                v.memset(ones[:, :], 1.0).then_inc(s_const, 1)
                v.memset(hpad[:, :, 0:F], 0.0).then_inc(s_const, 1)
                v.memset(gat[:, :, :, :], 0.0).then_inc(s_const, 1)
                v.memset(cT[:, N:N + WIN + 64], 0.0).then_inc(s_const, 1)
                v.wait_ge(s_iota, 2)
                v.tensor_scalar(ident[:, :], iot[:, :], 0.0, None, ALU.is_equal).then_inc(s_const, 1)
                v.tensor_copy(winf[:, :, :], wint[:, :, :]).then_inc(s_const, 1)
                v.wait_ge(s_w, WL)
                for k, w in enumerate((w1n[F:2 * F, :], w1e[:, :], b1r[:, :])):
                    p = w.shape[0]
                    lo = F if k == 0 else 0
                    m = wmean[lo:lo + p, k:k + 1]
                    v.tensor_reduce(m, w, X, ALU.add).then_inc(s_dstep, 1)
                    v.wait_ge(s_dstep, 3 * k + 1)
                    v.tensor_scalar(m, m, 1.0 / F, None, ALU.mult).then_inc(s_dstep, 1)
                    v.wait_ge(s_dstep, 3 * k + 2)
                    v.tensor_scalar(w, w, m, None, ALU.subtract).then_inc(s_dstep, 1)
                for c in range(BC):
                    v.tensor_copy(b2rep[:, c, :], rows[:, 0, :]).then_inc(s_const, 1)
                v.wait_ge(s_x, 16)
                def chunk(g):
                    xg = xs[:, bass.ds(g * CH, CH), :]
                    v.tensor_reduce(stat[:, 0, :], xg, X, ALU.add).then_inc(s_norm, 1)
                    wait(v, s_norm, NORM * g + 1)
                    v.tensor_scalar(stat[:, 1, :], stat[:, 0, :], 1.0 / F, None, ALU.mult).then_inc(s_norm, 1)
                    wait(v, s_norm, NORM * g + 2)
                    wait(v, s_pad, g)
                    v.tensor_tensor(xc[:, :, :], xg, bcast(stat[:, 1, :], F), ALU.subtract).then_inc(s_cen, 1)
                    wait(v, s_sqd, g + 1)
                    v.tensor_reduce(stat[:, 2, :], sqc[:, :, :], X, ALU.add).then_inc(s_norm, 1)
                    wait(v, s_norm, NORM * g + 3)
                    rstd(v, stat[:, 2, :], stat[:, 3, :], stat[:, 0, :], s_norm, NORM * g + 3)
                    wait(v, s_cen, 2 * g + 1)
                    v.tensor_tensor(xc[:, :, :], xc[:, :, :], bcast(stat[:, 3, :], F), ALU.mult).then_inc(s_cen, 1)
                repeated(v, CHUNKS, chunk)
                v.wait_ge(s_i, 32)
                v.tensor_copy(base_int[:, :], dst_all[0:1, :, 0]).then_inc(s_dstep, 1)
                v.tensor_copy(base_row[:, :], dst_all[0:1, :, 0]).then_inc(s_dstep, 1)
                for k in range(0, BLOCKS, 512):
                    n = min(512, BLOCKS - k)
                    v.wait_ge(s_bp, k // 512 + 1)
                    v.tensor_tensor(rel_all[:, k:k + n, :], dst_all[:, k:k + n, :],
                                    bcast(ag[k // 512][:, 0:n], BC), ALU.subtract).then_inc(s_dstep, 1)
                nb = 11 + -(-BLOCKS // 512)
                v.wait_ge(s_dstep, nb)
                flat = rel_all[:, :, :].rearrange("p b c -> p (b c)")
                v.tensor_reduce(worst[:, 0:1], flat, X, ALU.max).then_inc(s_dstep, 1)
                v.tensor_reduce(worst[:, 1:2], flat, X, ALU.min).then_inc(s_dstep, 1)
                v.wait_ge(s_dstep, nb + 2)
                v.tensor_scalar(worst[:, 0:1], worst[:, 0:1], float(WIN - 1), None, ALU.subtract).then_inc(s_dstep, 1)
                v.tensor_scalar(worst[:, 1:2], worst[:, 1:2], -1.0, None, ALU.mult).then_inc(s_dstep, 1)
                v.wait_ge(s_dstep, nb + 4)
                v.tensor_tensor(worst[:, 2:3], worst[:, 0:1], worst[:, 1:2], ALU.max).then_inc(s_dstep, 1)
                v.wait_ge(s_wt, 1)
                v.tensor_reduce(worst_row[:, :], zp[0][0:1, 0:128], X, ALU.max).then_inc(s_dstep, 1)
                v.wait_ge(s_dstep, nb + 6)
                v.tensor_scalar(flag[:, :], worst_row[:, :], 0.0, None, ALU.is_gt).then_inc(s_dstep, 1)
                v.wait_ge(s_bp, 1 + -(-BLOCKS // 512))
                v.tensor_copy(gb[:, :, :], zp[1][:, 0:2 * F].rearrange("p (k f) -> p k f", k=2)).then_inc(s_dstep, 1)

            @block.scalar
            def _(a):
                a.wait_ge(s_const, 7)
                def chunk(g):
                    wait(a, s_cen, 2 * g + 1)
                    a.activation(sqc[:, :, :], xc[:, :, :], ACT.Square).then_inc(s_sqd, 1)
                    wait(a, s_cen, 2 * g + 2)
                    wait(a, s_padfree, g + 1)
                    a.activation(hpad[:, :, F:2 * F], xc[:, :, :], ACT.Relu).then_inc(s_pad, 1)
                    for q in range(BQ):
                        wait(a, s_tr, BQ * g + q + 1)
                        wait(a, s_cT, BQ * g + max(q - 1, 0))
                        a.activation(cols[:, q % 2, :], tp[q % 2][:, 0:Q * TP], ACT.Copy).then_inc(s_cp, 1)
                        wait(a, s_pr, BQ * g + q + 1)
                        if q == 0:
                            wait(a, s_ps, 16 * g)
                        a.activation(prow[:, q * Q:(q + 1) * Q, :],
                                     mp[q % 2][0:TP, 0:Q * F].rearrange("p (t f) -> p t f", t=Q),
                                     ACT.Copy).then_inc(s_prc, 1)
                repeated(a, CHUNKS, chunk)

            @block.tensor
            def _(pe):
                pe.sem_inc(s_padfree, 1)
                pe.wait_ge(s_const, 7)
                pe.wait_ge(s_dstep, 9)
                def chunk(g):
                    wait(pe, s_pad, g + 1)
                    for q in range(BQ):
                        for t in range(Q):
                            mm = pe.transpose(tp[q % 2][:, t * TP:(t + 1) * TP], hpad[:, q * Q + t, :],
                                              ident[0:TP, 0:TP])
                        mm.then_inc(s_tr, 1)
                        wait(pe, s_cp, BQ * g + q + 1)
                        for t in range(Q):
                            o = mp[q % 2][0:TP, t * F:(t + 1) * F]
                            pe.matmul(o, ones[:, 0:TP], b1r[:, :], start=True, stop=False)
                            mm = pe.matmul(o, cols[F:2 * F, q % 2, t * TP:(t + 1) * TP],
                                           w1n[F:2 * F, :], start=False, stop=True)
                        mm.then_inc(s_pr, 1)
                        wait(pe, s_prc, BQ * g + q + 1)
                    pe.sem_inc(s_padfree, 1)
                repeated(pe, CHUNKS, chunk)
                pe.wait_ge(s_dstep, 11)
                for k in range(0, BLOCKS, 512):
                    n = min(512, BLOCKS - k)
                    pe.matmul(ag[k // 512][:, 0:n], ones[:, :], base_row[:, k:k + n],
                              start=True, stop=True).then_inc(s_bp, 1)
                pe.matmul(zp[1][:, 0:2 * F], ones[:, :], rows[:, 2:4, :].rearrange("o k f -> o (k f)"),
                          start=True, stop=True).then_inc(s_bp, 1)
                pe.wait_ge(s_dstep, 11 + -(-BLOCKS // 512) + 5)
                pe.transpose(zp[0][0:1, 0:128], worst[:, 2:3], ident[:, :]).then_inc(s_wt, 1)

        def gather(pool, table, n, j, done):
            for c in range(BC):
                pool.indirect_dma_start(
                    out=gat[:, j, c, :], out_offset=None, in_=table[:, :],
                    in_offset=bass.IndirectOffsetOnAxis(ap=idx[:, j, c:c + 1], axis=0)).then_inc(done, 16)

        def edge_products(pe, j):
            for c in range(BC):
                mm = pe.matmul(zp[j % 2][:, c * F:(c + 1) * F], ea[:, j, c * 128:(c + 1) * 128], w1e[:, :],
                               start=True, stop=True)
            return mm

        def transposes(pe, j):
            for k in range(PAIRS):
                mm = pe.transpose(tp[j % 2][:, k * 128:(k + 1) * 128],
                                  gat[:, j, 2 * k:2 * k + 2, :].rearrange("p c f -> p (c f)"), ident[:, :])
            return mm

        def second_products(pe, j):
            o = mp[j % 2]
            pe.matmul(o[:, 0:BC * F], ones[:, :], b2rep[:, :, :].rearrange("o c f -> o (c f)"),
                      start=True, stop=False, skip_group_check=True)
            for k in range(BC // 2):
                mm = pe.matmul(o[:, k * 128:(k + 1) * 128], hT[:, j, k * 128:(k + 1) * 128], w2d[:, :],
                               start=False, stop=(k == PAIRS - 1), skip_group_check=True)
            if BC % 2:
                k = BC // 2
                mm = pe.matmul(o[:, k * 128:k * 128 + F], hT[0:F, j, k * 128:(k + 1) * 128],
                               w2d[0:F, 0:F], start=False, stop=True, skip_group_check=True)
            return mm

        def window_sums(pe, j, rows_of):
            for c in range(BC):
                mm = pe.matmul(ag[j % 2][0:F, 0:WIN], rows_of[:, c, :], oh[:, j, c, :],
                               start=(c == 0), stop=(c == BC - 1))
            return mm

        def one_hot(v, j, rel):
            return v.tensor_tensor(oh[:, j, :, :], winf[:, :, :], bcast(rel, WIN), ALU.is_equal)

        def block_of(t, n):
            return t[:, n, :] if isinstance(n, int) else t[:, bass.ds(n, 1), :].rearrange("p o c -> p (o c)")

        def edge_of(n):
            return edge_t[n, :, :] if isinstance(n, int) else edge_t[bass.ds(n, 1), :, :].rearrange("o k e -> (o k) e")

        def indices(a, n, j):
            return a.activation(idx[:, j, :], block_of(src_all, n), ACT.Copy)

        def add_sums(v, n, j):
            b = v.value_load(base_int[0:1, bass.ds(n, 1)], min_val=0, max_val=N)
            to = cT[0:F, bass.ds(b, WIN)]
            return v.tensor_tensor(to, to, ag[j % 2][0:F, 0:WIN], ALU.add)

        def before(j):
            return 1 if j == 0 else 2

        def lagged(r, j, lag):
            r2, j2 = r + (j - lag) // UN, (j - lag) % UN
            return r2, j2, r2 * UN + j2

        def there(n):
            return not isinstance(n, int) or 0 <= n < BLOCKS

        def rounds(eng, step, lag, lead=1):
            for j in range(lead * UN):
                step(j // UN, j % UN)
            with eng.Fori(lead, ROUNDS - 1) as r:
                for j in range(UN):
                    step(r, j)
            for j in range(UN + lag):
                step(ROUNDS - 1, j)

        def flagged(eng):
            return eng.value_load(flag[0:1, 0:1], min_val=0, max_val=1)

        g_idx = sem("l0_index_ready")
        g_ea = [sem(f"l0_edges_loaded{j}") for j in range(UN)]
        g_gat = [sem(f"l0_rows_gathered{j}") for j in range(UN)]
        g_ep = sem("l0_edge_products")
        g_z = sem("l0_z_ready")
        g_sq = sem("l0_z_squared")
        g_red = sem("l0_squares_summed")
        g_rs = sem("l0_rstd_ready")
        g_n = sem("l0_z_normalised")
        g_t = sem("l0_z_transposed")
        g_h = sem("l0_hidden_ready")
        g_m = sem("l0_second_products")
        g_msg = sem("l0_messages_ready")
        g_oh = sem("l0_one_hot_ready")
        g_sum = sem("l0_window_summed")
        g_add = sem("l0_sums_added")

        with nc.Block() as block:
            @block.sync
            def _(sp):
                def step(r, j):
                    n = r * UN + j
                    wait(sp, g_ep, n - UN + 1)
                    sp.dma_start(ea[:, j, :], edge_of(n)).then_inc(g_ea[j], 16)
                with sp.If(flagged(sp) == 0):
                    rounds(sp, step, 0)

            @block.gpsimd
            def _(pool):
                def step(r, j):
                    n = r * UN + j
                    wait(pool, g_idx, n + 1)
                    wait(pool, g_t, n - UN + 1)
                    wait_alone(pool, "gpsimd")
                    gather(pool, ptab, n, j, g_gat[j])
                with pool.If(flagged(pool) == 0):
                    rounds(pool, step, 0)

            @block.tensor
            def _(pe):
                def step(r, j):
                    _, s, n = lagged(r, j, 1)
                    if there(n):
                        wait(pe, g_n, n + 1)
                        wait(pe, g_h, n + 1 - before(s))
                        transposes(pe, s).then_inc(g_t, 1)
                    _, s, n = lagged(r, j, 2)
                    if there(n):
                        wait(pe, g_h, n + 1)
                        wait(pe, g_msg, n + 1 - before(s))
                        second_products(pe, s).then_inc(g_m, 1)
                    q, s, n = lagged(r, j, -1)
                    if there(n):
                        wait(pe, g_ea[s], q * 16 + 16)
                        wait(pe, g_z, n + 1 - before(s))
                        edge_products(pe, s).then_inc(g_ep, 1)
                    _, s, n = lagged(r, j, 3)
                    if there(n):
                        wait(pe, g_msg, n + 1)
                        wait(pe, g_oh, n + 1)
                        wait(pe, g_add, n + 1 - before(s))
                        window_sums(pe, s, msg[:, s, :, :]).then_inc(g_sum, 1)
                with pe.If(flagged(pe) == 0):
                    pe.wait_ge(g_ea[0], 16)
                    edge_products(pe, 0).then_inc(g_ep, 1)
                    rounds(pe, step, 3)

            @block.scalar
            def _(a):
                def step(r, j):
                    _, s, n = lagged(r, j, 0)
                    if there(n):
                        wait(a, g_z, n + 1)
                        wait(a, g_red, n + 1 - before(s))
                        a.activation(sq[:, s % 2, :, :], gat[:, s, 0:BC, :], ACT.Square).then_inc(g_sq, 1)
                        if there(n + UN):
                            indices(a, n + UN, s).then_inc(g_idx, 1)
                    _, s, n = lagged(r, j, 1)
                    if there(n):
                        wait(a, g_t, n + 1)
                        wait(a, g_m, n + 1 - UN)
                        a.activation(hT[:, s, :], tp[s % 2][:, 0:PAIRS * 128], ACT.Silu,
                                     bias=gcol[:, 1:2], scale=gcol[:, 0:1]).then_inc(g_h, 1)
                    _, s, n = lagged(r, j, 2)
                    if there(n):
                        wait(a, g_m, n + 1)
                        wait(a, g_sum, n + 1 - UN)
                        a.activation(msg[:, s, :, :], mp[s % 2][:, 0:BC * F].rearrange("p (c f) -> p c f", c=BC),
                                     ACT.Silu).then_inc(g_msg, 1)
                with a.If(flagged(a) == 0):
                    for j in range(UN):
                        indices(a, j, j).then_inc(g_idx, 1)
                    rounds(a, step, 2, lead=2)

            @block.vector
            def _(v):
                def step(r, j):
                    q, s, n = lagged(r, j, 0)
                    z = gat[:, s, 0:BC, :]
                    if there(n):
                        wait(v, g_ep, n + 1)
                        wait(v, g_gat[s], q * (16 * BC) + 16 * BC)
                        v.tensor_tensor(z, zp[s % 2][:, 0:BC * F].rearrange("p (c f) -> p c f", c=BC), z,
                                        ALU.add).then_inc(g_z, 1)
                        wait(v, g_sum, n + 1 - UN)
                        one_hot(v, s, block_of(rel_all, n)).then_inc(g_oh, 1)
                    _, t, m = lagged(r, j, 4)
                    if there(m):
                        wait(v, g_sum, m + 1)
                        wait(v, g_add, m)
                        add_sums(v, m, t).then_inc(g_add, 1)
                    if there(n):
                        wait(v, g_sq, n + 1)
                        v.tensor_reduce(st[:, 0, 0, :], sq[:, s % 2, :, :], X, ALU.add).then_inc(g_red, 1)
                        wait(v, g_red, n + 1)
                        rstd(v, st[:, 0, 0, :], st[:, 1, 0, :], st[:, 0, 1, :], g_rs, n * RSTD)
                        v.tensor_tensor(z, z, bcast(st[:, 1, 0, :], F), ALU.mult).then_inc(g_n, 1)
                with v.If(flagged(v) == 0):
                    rounds(v, step, 4)

        def general(layer, table):
            def gsem(name):
                return sem(f"general{layer}_{name}")
            x_done, x_idx, x_ea, x_gat, x_ep = map(gsem, ("block_done", "index_ready", "edges_loaded", "rows_gathered", "edge_products"))
            x_z, x_sq, x_st, x_n, x_t = map(gsem, ("z_ready", "squared", "rstd_steps", "normalised", "transposed"))
            x_h, x_m, x_msg, x_rel, x_oh = map(gsem, ("hidden_ready", "second_products", "messages_ready", "window_steps", "one_hot_ready"))
            x_sum, x_add = map(gsem, ("window_summed", "sums_added"))

            def sync(sp):
                if layer == 0:
                    with sp.Fori(0, BLOCKS) as n:
                        sp.wait_ge(x_done, n + 1)
                        sp.dma_start(ea[:, 0, :], edge_of(n)).then_inc(x_ea, 16)

            def gpsimd(pool):
                with pool.Fori(0, BLOCKS) as n:
                    pool.wait_ge(x_idx, n + 1)
                    wait_alone(pool, "gpsimd")
                    gather(pool, table, n, 0, x_gat)

            def scalar(a):
                with a.Fori(0, BLOCKS) as n:
                    a.wait_ge(x_done, n + 1)
                    indices(a, n, 0).then_inc(x_idx, 1)
                    if layer == 0:
                        a.wait_ge(x_z, n + 1)
                        a.activation(sq[:, 0, :, :], gat[:, 0, 0:BC, :], ACT.Square).then_inc(x_sq, 1)
                        a.wait_ge(x_t, n + 1)
                        a.activation(hT[:, 0, :], tp[0][:, 0:PAIRS * 128], ACT.Silu,
                                     bias=gcol[:, 1:2], scale=gcol[:, 0:1]).then_inc(x_h, 1)
                        a.wait_ge(x_m, n + 1)
                        a.activation(msg[:, 0, :, :], mp[0][:, 0:BC * F].rearrange("p (c f) -> p c f", c=BC),
                                     ACT.Silu).then_inc(x_msg, 1)

            def tensor(pe):
                with pe.Fori(0, BLOCKS) as n:
                    if layer == 0:
                        pe.wait_ge(x_ea, 16 * n + 16)
                        pe.wait_ge(x_done, n + 1)
                        edge_products(pe, 0).then_inc(x_ep, 1)
                        pe.wait_ge(x_n, n + 1)
                        transposes(pe, 0).then_inc(x_t, 1)
                        pe.wait_ge(x_h, n + 1)
                        second_products(pe, 0).then_inc(x_m, 1)
                        pe.wait_ge(x_msg, n + 1)
                    else:
                        pe.wait_ge(x_gat, n * (16 * BC) + 16 * BC)
                    wait_alone(pe, "tensor")
                    with pe.Fori(0, WINDOWS) as w:
                        k = n * WINDOWS + w
                        pe.wait_ge(x_oh, k + 1)
                        pe.wait_ge(x_add, k + 1)
                        window_sums(pe, 0, msg[:, 0, :, :] if layer == 0 else gat[:, 0, 0:BC, :]).then_inc(x_sum, 1)

            def vector(v):
                v.sem_inc(x_done, 1)
                v.sem_inc(x_sum, 1)
                v.sem_inc(x_add, 1)
                with v.Fori(0, BLOCKS) as n:
                    v.memset(wbase[:, :], 0.0).then_inc(x_rel, 1)
                    if layer == 0:
                        v.wait_ge(x_ep, n + 1)
                        v.wait_ge(x_gat, n * (16 * BC) + 16 * BC)
                        z = gat[:, 0, 0:BC, :]
                        v.tensor_tensor(z, zp[0][:, 0:BC * F].rearrange("p (c f) -> p c f", c=BC), z,
                                        ALU.add).then_inc(x_z, 1)
                        v.wait_ge(x_sq, n + 1)
                        v.tensor_reduce(st[:, 0, 0, :], sq[:, 0, :, :], X, ALU.add).then_inc(x_st, 1)
                        v.wait_ge(x_st, n * (RSTD + 1) + 1)
                        rstd(v, st[:, 0, 0, :], st[:, 1, 0, :], st[:, 0, 1, :], x_st, n * (RSTD + 1) + 1)
                        v.tensor_tensor(z, z, bcast(st[:, 1, 0, :], F), ALU.mult).then_inc(x_n, 1)
                    with v.Fori(0, WINDOWS) as w:
                        k = n * WINDOWS + w
                        v.wait_ge(x_rel, k * 2 + n + 1)
                        v.tensor_scalar(reln[:, :], block_of(dst_all, n), wbase[:, :], None, ALU.subtract).then_inc(x_rel, 1)
                        v.wait_ge(x_rel, k * 2 + n + 2)
                        v.wait_ge(x_sum, k + 1)
                        one_hot(v, 0, reln[:, :]).then_inc(x_oh, 1)
                        v.tensor_scalar(wbase[:, :], wbase[:, :], float(WIN), None, ALU.add).then_inc(x_rel, 1)
                        v.wait_ge(x_sum, k + 2)
                        v.wait_ge(x_add, k + 1)
                        to = cT[0:F, bass.ds(w * WIN, WIN)]
                        v.tensor_tensor(to, to, ag[0][0:F, 0:WIN], ALU.add).then_inc(x_add, 1)
                    v.wait_ge(x_add, n * WINDOWS + WINDOWS + 1)
                    v.wait_ge(x_oh, n * WINDOWS + WINDOWS)
                    v.sem_inc(x_done, 1)

            with nc.Block() as block:
                @block.sync
                def _(sp):
                    with sp.If(flagged(sp) != 0):
                        sync(sp)

                @block.gpsimd
                def _(pool):
                    with pool.If(flagged(pool) != 0):
                        gpsimd(pool)

                @block.tensor
                def _(pe):
                    with pe.If(flagged(pe) != 0):
                        tensor(pe)

                @block.scalar
                def _(a):
                    with a.If(flagged(a) != 0):
                        scalar(a)

                @block.vector
                def _(v):
                    with v.If(flagged(v) != 0):
                        vector(v)

        general(0, ptab)

        u_w = sem("update_columns_ready")
        u_u = sem("update_products")
        u_s = sem("update_ready")
        u_v = sem("update_vector_steps")
        u_c = sem("update_centred")
        u_q = sem("update_squared")
        u_h = sem("layer1_h_ready")
        u_st = sem("layer1_rows_stored")
        u_t = sem("layer1_transposed")
        u_cp = sem("layer1_columns_copied")

        with nc.Block() as block:
            @block.gpsimd
            def _(pool):
                def chunk(g):
                    for q in range(BQ):
                        wait(pool, u_u, BQ * g + max(q - 1, 0))
                        pool.tensor_copy(cols[:, q % 2, :],
                                         cT[:, bass.ds(g * (CH * TP) + q * Q * TP, Q * TP)]).then_inc(u_w, 1)
                repeated(pool, CHUNKS, chunk)

            @block.tensor
            def _(pe):
                def chunk(g):
                    for q in range(BQ):
                        wait(pe, u_w, BQ * g + q + 1)
                        wait(pe, u_s, BQ * g + max(q - 1, 0))
                        for t in range(Q):
                            o = mp[q % 2][0:TP, t * F:(t + 1) * F]
                            pe.matmul(o, ones[:, 0:TP], rows[:, 1, :], start=True, stop=False)
                            mm = pe.matmul(o, cols[:, q % 2, t * TP:(t + 1) * TP], wu[:, :],
                                           start=False, stop=True)
                        mm.then_inc(u_u, 1)
                    wait(pe, u_h, g + 1)
                    for q in range(BQ):
                        wait(pe, u_cp, BQ * g + max(q - 1, 0))
                        wait_alone(pe, "tensor")
                        for t in range(Q):
                            mm = pe.transpose(tp[q % 2][0:F, t * TP:(t + 1) * TP], prow[:, q * Q + t, :],
                                              ident[0:TP, 0:TP])
                        mm.then_inc(u_t, 1)
                repeated(pe, CHUNKS, chunk)

            @block.scalar
            def _(a):
                def chunk(g):
                    for q in range(BQ):
                        wait(a, u_u, BQ * g + q + 1)
                        wait(a, u_v, g * (2 * NORM + 2))
                        a.activation(xc[:, q * Q:(q + 1) * Q, :],
                                     mp[q % 2][0:TP, 0:Q * F].rearrange("p (t f) -> p t f", t=Q),
                                     ACT.Silu).then_inc(u_s, 1)
                    for k in range(2):
                        wait(a, u_c, 2 * g + k + 1)
                        a.activation(sqc[:, :, :], xc[:, :, :], ACT.Square).then_inc(u_q, 1)
                    wait(a, u_v, g * (2 * NORM + 2) + 2 * NORM + 2)
                    wait(a, u_st, 16 * g)
                    wait(a, u_t, BQ * g)
                    a.activation(prow[:, :, :], xc[:, :, :], ACT.Relu).then_inc(u_h, 1)
                    for q in range(BQ):
                        wait(a, u_t, BQ * g + q + 1)
                        a.activation(cT[0:F, bass.ds(g * (CH * TP) + q * Q * TP, Q * TP)],
                                     tp[q % 2][0:F, 0:Q * TP], ACT.Copy).then_inc(u_cp, 1)
                repeated(a, CHUNKS, chunk)

            @block.vector
            def _(v):
                def norm(base, g, k):
                    v.tensor_reduce(stat[:, 0, :], xc[:, :, :], X, ALU.add).then_inc(u_v, 1)
                    v.wait_ge(u_v, base + 1)
                    v.tensor_scalar(stat[:, 1, :], stat[:, 0, :], 1.0 / F, None, ALU.mult).then_inc(u_v, 1)
                    v.wait_ge(u_v, base + 2)
                    v.tensor_tensor(xc[:, :, :], xc[:, :, :], bcast(stat[:, 1, :], F), ALU.subtract).then_inc(u_c, 1)
                    v.wait_ge(u_q, 2 * g + k + 1)
                    v.tensor_reduce(stat[:, 2, :], sqc[:, :, :], X, ALU.add).then_inc(u_v, 1)
                    v.wait_ge(u_v, base + 3)
                    rstd(v, stat[:, 2, :], stat[:, 3, :], stat[:, 0, :], u_v, base + 3)
                    v.wait_ge(u_c, 2 * g + k + 1)
                    v.tensor_tensor(xc[:, :, :], xc[:, :, :], bcast(stat[:, 3, :], F), ALU.mult).then_inc(u_v, 1)

                u_x = sem("residual_steps")
                def chunk(g):
                    wait(v, u_s, BQ * g + BQ)
                    norm(g * (2 * NORM + 2), g, 0)
                    wait(v, u_v, g * (2 * NORM + 2) + NORM + 1)
                    v.tensor_tensor(xc[:, :, :], xc[:, :, :], per_tile(gb[0:TP, 0, :], CH), ALU.mult).then_inc(u_x, 1)
                    wait(v, u_x, 4 * g + 1)
                    v.tensor_tensor(xc[:, :, :], xc[:, :, :], per_tile(gb[0:TP, 1, :], CH), ALU.add).then_inc(u_x, 1)
                    wait(v, u_x, 4 * g + 2)
                    xg = xs[:, bass.ds(g * CH, CH), :]
                    v.tensor_tensor(xc[:, :, :], xg, xc[:, :, :], ALU.add).then_inc(u_x, 1)
                    wait(v, u_x, 4 * g + 3)
                    v.tensor_scalar(xg, xc[:, :, :], 1.0, None, ALU.mult).then_inc(u_x, 1)
                    wait(v, u_x, 4 * g + 4)
                    norm(g * (2 * NORM + 2) + NORM + 1, g, 1)
                    wait(v, u_h, g + 1)
                repeated(v, CHUNKS, chunk)

            @block.sync
            def _(sp):
                def chunk(g):
                    wait(sp, u_h, g + 1)
                    sp.dma_start(htab_t[:, bass.ds(g * CH, CH), :], prow[:, :, :]).then_inc(u_st, 16)
                repeated(sp, CHUNKS, chunk)
                sp.wait_ge(u_st, 16 * CHUNKS)

        k_idx = sem("l1_index_ready")
        k_gat = [sem(f"l1_rows_gathered{j}") for j in range(UN)]
        k_oh = sem("l1_one_hot_ready")
        k_sum = sem("l1_window_summed")
        k_add = sem("l1_sums_added")

        with nc.Block() as block:
            @block.gpsimd
            def _(pool):
                def step(r, j):
                    n = r * UN + j
                    wait(pool, k_idx, n + 1)
                    wait(pool, k_sum, n - UN + 1)
                    wait_alone(pool, "gpsimd")
                    gather(pool, htab, n, j, k_gat[j])
                with pool.If(flagged(pool) == 0):
                    rounds(pool, step, 0)

            @block.scalar
            def _(a):
                def step(r, j):
                    n = r * UN + j
                    wait(a, k_sum, n - UN + 1)
                    indices(a, n, j).then_inc(k_idx, 1)
                with a.If(flagged(a) == 0):
                    rounds(a, step, 0)

            @block.tensor
            def _(pe):
                def step(r, j):
                    n = r * UN + j
                    wait(pe, k_gat[j], r * (16 * BC) + 16 * BC)
                    wait(pe, k_oh, n + 1)
                    wait(pe, k_add, n + 1 - before(j))
                    window_sums(pe, j, gat[:, j, 0:BC, :]).then_inc(k_sum, 1)
                with pe.If(flagged(pe) == 0):
                    rounds(pe, step, 0)

            @block.vector
            def _(v):
                def step(r, j):
                    _, s, m = lagged(r, j, -1)
                    if there(m):
                        wait(v, k_sum, m + 1 - UN)
                        one_hot(v, s, block_of(rel_all, m)).then_inc(k_oh, 1)
                    n = r * UN + j
                    wait(v, k_sum, n + 1)
                    wait(v, k_add, n)
                    add_sums(v, n, j).then_inc(k_add, 1)
                with v.If(flagged(v) == 0):
                    one_hot(v, 0, block_of(rel_all, 0)).then_inc(k_oh, 1)
                    rounds(v, step, 0)

        general(1, htab)

        e_h = sem("mlp_hidden_products")
        e_r = sem("mlp_hidden_ready")
        e_o = sem("mlp_products")
        e_x = sem("result_ready")
        e_st = sem("result_stored")
        BATCHES = T // Q

        with nc.Block() as block:
            @block.tensor
            def _(pe):
                def batch(b):
                    wait(pe, e_r, HS * b)
                    for h in range(HS):
                        pe.matmul(tp[h][:, 0:Q * TP], m1[:, h * 128:(h + 1) * 128],
                                  cT[0:F, bass.ds(b * (Q * TP), Q * TP)], start=True, stop=True).then_inc(e_h, 1)
                    wait(pe, e_r, HS * b + HS)
                    wait(pe, e_x, b)
                    for t in range(Q):
                        o = mp[0][0:TP, t * F:(t + 1) * F]
                        pe.matmul(o, ones[:, 0:TP], rows[:, 4, :], start=True, stop=False)
                        for h in range(HS):
                            mm = pe.matmul(o, hid[:, h, t * TP:(t + 1) * TP], m2[:, h, :],
                                           start=False, stop=(h == HS - 1))
                    mm.then_inc(e_o, 1)
                repeated(pe, BATCHES, batch)

            @block.scalar
            def _(a):
                def batch(b):
                    for h in range(HS):
                        wait(a, e_h, HS * b + h + 1)
                        wait(a, e_o, b)
                        a.activation(hid[:, h, :], tp[h][:, 0:Q * TP], ACT.Relu, bias=c1col[:, h:h + 1]).then_inc(e_r, 1)
                repeated(a, BATCHES, batch)

            @block.vector
            def _(v):
                def batch(b):
                    wait(v, e_o, b + 1)
                    xb = xs[:, bass.ds(b * Q, Q), :]
                    v.tensor_tensor(xb, xb, mp[0][0:TP, 0:Q * F].rearrange("p (t f) -> p t f", t=Q),
                                    ALU.add).then_inc(e_x, 1)
                repeated(v, BATCHES, batch)

            @block.sync
            def _(sp):
                def batch(b):
                    wait(sp, e_x, b + 1)
                    sp.dma_start(out_t[:, bass.ds(b * Q, Q), :], xs[:, bass.ds(b * Q, Q), :]).then_inc(e_st, 16)
                repeated(sp, BATCHES, batch)
                sp.wait_ge(e_st, 16 * BATCHES)


BLOCK_COLUMNS = 5
INPUTS = ["x", "src", "dst", "edge_t", "L0_gnn_W1", "L0_gnn_b1", "L0_gnn_g1", "L0_gnn_be1", "L0_gnn_W2", "L0_gnn_b2",
          "L0_gnn_Wu", "L0_gnn_bu", "L0_gnn_gn", "L0_gnn_bn", "L1_gnn_W1", "L1_gnn_b1", "L1_gnn_W2", "L1_gnn_b2"]


def kernel(x, src, dst, edge_attr_32, **weights):
    import numpy as np
    import concourse.bacc as bacc
    from concourse.bass_utils import run_bass_kernel_spmd

    E, ED = edge_attr_32.shape
    edges = 128 * BLOCK_COLUMNS
    blocks = E // edges
    arrays = {"x": np.ascontiguousarray(x)}
    for name, a in (("src", src), ("dst", dst)):
        arrays[name] = np.ascontiguousarray(np.asarray(a).reshape(blocks, 128, BLOCK_COLUMNS).transpose(1, 0, 2))
    arrays["edge_t"] = np.ascontiguousarray(
        np.asarray(edge_attr_32).reshape(blocks, 128, BLOCK_COLUMNS, ED).transpose(0, 3, 2, 1)
        .reshape(blocks, ED, edges))
    for name, a in weights.items():
        arrays[name] = np.ascontiguousarray(a)

    nc = bacc.Bacc("TRN2", target_bir_lowering=False, num_devices=1)
    args = [nc.dram_tensor(f"in_{n}", arrays[n].shape, mybir.dt.from_np(arrays[n].dtype), kind="ExternalInput").ap()
            for n in INPUTS]
    out = nc.dram_tensor("out", arrays["x"].shape, mybir.dt.float32, kind="ExternalOutput").ap()
    build_gnn(nc, *args, out)
    r = run_bass_kernel_spmd(nc, [{f"in_{n}": arrays[n] for n in INPUTS}], core_ids=[0])
    return r.results[0]["out"]
```

```python
import concourse.bass as bass
from concourse import mybir
from contextlib import ExitStack


def build_gnn(nc, x, src, dst, src_dense, dst_dense, edge_pairs, edge_last, W1, b1, g1, be1, W2, b2, Wu, bu, gn, bn, M1, c1, M2, c2, out):
    f32, bf16, f16, i32 = mybir.dt.float32, mybir.dt.bfloat16, mybir.dt.float16, mybir.dt.int32
    ALU = mybir.AluOpType
    ACT = mybir.ActivationFunctionType
    X = mybir.AxisListType.X
    XY = mybir.AxisListType.XY
    EPS = 1e-5

    N, F = x.shape
    ED = edge_last.shape[1]
    BLOCKS, BC = src.shape[1], src.shape[2]
    EB = 128 * BC
    UN = 5
    ROUNDS = BLOCKS // UN
    WIN = 64
    WINDOWS = -(-N // WIN)
    H = M1.shape[1]
    HS = H // 128
    TP = max(t for t in range(1, 129) if N % t == 0)
    T = N // TP
    Q = 4
    CH = 20 if T % 20 == 0 else Q
    CHUNKS = T // CH
    BQ = CH // Q
    PAIRS = -(-BC // 2)
    DENSE, GC = src_dense.shape[1], src_dense.shape[2]
    GP = -(-GC // 2)
    PW = 12
    GW = 128
    BANKS = -(-BLOCKS // 512)
    PER = 512 // GP
    GBANKS = -(-DENSE // PER)
    G0 = ROUNDS - DENSE
    assert GC == UN * BC and G0 == DENSE + 1 and 4 * T <= 512 and PW == 12
    assert BC % 2 == 1 and BLOCKS % UN == 0 and T % CH == 0 and CH % Q == 0 and F == 64 and ED == 32 and TP * Q <= 512

    ctx = ExitStack()
    with ctx:
        def sb(name, shape, dt=f32):
            return ctx.enter_context(nc.sbuf_tensor(name, shape, dt))

        def region(name, size):
            left = [sb(name, [128, size // 4]), 0]

            def view(shape, dt=f32):
                count = 1
                for n in shape[1:]:
                    count *= n
                words = (count * (2 if dt in (bf16, f16) else 4) + 3) // 4
                part = left[0][0:shape[0], left[1]:left[1] + words]
                left[1] += words
                assert left[1] <= size // 4, (name, left[1] * 4, size)
                if dt != f32:
                    part = part.bitcast(dt)[:, 0:count]
                if len(shape) > 2:
                    names = "abcd"[:len(shape) - 1]
                    part = part.rearrange(f"p ({' '.join(names)}) -> p {' '.join(names)}",
                                          **{k: n for k, n in zip(names[:-1], shape[1:-1])})
                return part

            def again():
                left[1] = 0
            return view, again

        def sem(name):
            return ctx.enter_context(nc.semaphore(name))

        ptab = nc.dram_tensor("layer0_rows", (N, F), f32, kind="Internal").ap()
        htab = nc.dram_tensor("layer1_rows", (N, F), f32, kind="Internal").ap()

        xs = sb("xs", [TP, T, F])
        cT = sb("cT", [128, N + GW])
        src_all = sb("src_all", [128, BLOCKS, BC], i32)
        rel_all = sb("rel_all", [128, BLOCKS, BC], bf16)
        base_int = sb("base_int", [1, BLOCKS], i32)
        flag = sb("flag", [1, 1], i32)
        worst = sb("worst", [128, 8])
        worst_row = sb("worst_row", [1, 1])
        number_i = sb("number_i", [128, 1], i32)
        number = sb("number", [128, 1])
        keys_all = sb("keys_all", [128, DENSE + 1, 2 * GC], f16)
        keys = sb("keys", [128, 2 * GC])
        held_all = sb("held_all", [128, DENSE])
        at_int = sb("at_int", [1, DENSE, GP], i32)

        w1n = sb("w1n", [128, F])
        w1e = sb("w1e", [2 * ED, 2 * F])
        b1r = sb("b1r", [1, F])
        wmean = sb("wmean", [128, 4])
        w2d = sb("w2d", [128, 128])
        wu = sb("wu", [128, F])
        m1 = sb("m1", [F, H])
        m2 = sb("m2", [128, HS, F])
        gcol = sb("gcol", [128, 2])
        c1col = sb("c1col", [128, HS])
        rows = sb("rows", [1, 5, F])
        b2rep = sb("b2rep", [3, BC, F], bf16)
        ones_b = sb("ones_b", [3, 128], bf16)
        gb = sb("gb", [128, 2, F])
        ones = sb("ones", [1, 128])
        ident = sb("ident", [128, 128])
        winf = sb("winf", [128, BC, WIN], bf16)
        keyf = sb("keyf", [128, PW * T], f16)
        lowf = sb("lowf", [128, TP], f16)
        wbase = sb("wbase", [128, 1])
        reln = sb("reln", [128, BC])
        dst_n = sb("dst_n", [128, BC], i32)
        stat = sb("stat", [TP, 4, CH])

        idx = sb("idx", [128, UN, BC], i32)
        gat = sb("gat", [128, UN, BC, F])
        oh = sb("oh", [128, UN, BC, WIN])
        st = sb("st", [128, UN, 3, BC])

        view, again = region("node_buffers", 42048)
        xc = view([TP, CH, F])
        sqc = view([TP, CH, F])
        prow = view([TP, CH, F])
        cols = view([128, 2, Q * TP])
        hpad = view([TP, CH, 2 * F])
        again()
        key_i = view([128, max(PW * T, TP)], i32)
        wint = view([128, BC, WIN], i32)
        iot = view([128, 128], i32)
        again()
        hid = view([128, HS, Q * TP])
        again()
        OHS = 5
        raw = view([128, 3 * F])
        cnt = view([TP, (GW + PW) * T], bf16)
        ohk = view([128, OHS, PW * T], bf16)
        ohl = view([128, OHS, 128], bf16)

        view, again = region("edge_buffers", max(3 * F * T * 2, 38400))
        dst_all = view([128, BLOCKS, BC], i32)
        src_d = view([128, DENSE, GC], i32)
        dst_d = view([128, DENSE, GC], i32)
        base_row = view([1, BLOCKS])
        pair_row = view([1, DENSE, GP])
        base_all = view([128, BLOCKS])
        b2part = view([1, 3, F], bf16)
        b2left = view([1, 2, F])
        offs = view([128, DENSE, GP])
        again()
        key_f = view([128, DENSE, GC])
        low_f = view([128, DENSE, GC])
        again()
        ea = view([2 * ED, UN, PAIRS * 128])
        zb = view([128, UN, BC, F])
        zn = view([128, 2, 2 * PAIRS, F])
        sq = view([128, 2, BC, F])
        hT = view([128, UN, PAIRS * 128])
        msg = view([128, UN, BC, F])
        again()
        hparts = view([TP, T, 3, F], bf16)

        ps = ctx.enter_context(nc.psum_tensor("ps", [128, 8, 512], f32))
        zp, tp, mp, ag = ([ps[:, 2 * k + i, :] for i in range(2)] for k in range(4))

        x_t = x.rearrange("(t p) f -> p t f", p=TP)
        out_t = out.rearrange("(t p) f -> p t f", p=TP)
        ptab_t = ptab.rearrange("(t p) f -> p t f", p=TP)
        htab_t = htab.rearrange("(t p) f -> p t f", p=TP)

        def bcast(a, n):
            return a.unsqueeze(2).broadcast_to([a.shape[0], a.shape[1], n])

        def per_tile(a, n):
            return a.unsqueeze(1).broadcast_to([a.shape[0], n, a.shape[1]])

        NORM = 15
        def wait(eng, semaphore, value):
            if not isinstance(value, int) or value > 0:
                eng.wait_ge(semaphore, value)

        def repeated(eng, count, body):
            body(0)
            with eng.Fori(1, count) as g:
                body(g)

        turns = {}

        def wait_alone(eng, name):
            if name not in turns:
                turns[name] = sem(f"turns_of_{name}")
            eng.sem_inc(turns[name], 1)

        HALF = 6
        RSTD = 12

        def rstd_step(v, k, total, y, t):
            if k == 0:
                return v.tensor_scalar(total, total, 1.0 / F, EPS, ALU.mult, ALU.add)
            if k == 1:
                return v.tensor_scalar(t.bitcast(i32), total.bitcast(i32), 1, None, ALU.logical_shift_right)
            if k == 2:
                return v.tensor_scalar(y.bitcast(i32), t.bitcast(i32), -1.0, float(0x5F3759DF), ALU.mult, ALU.add)
            if k % 3 == 0:
                return v.scalar_tensor_tensor(t, y, -0.5, y, ALU.mult, ALU.mult)
            if k % 3 == 1:
                return v.tensor_tensor(t, t, total, ALU.mult)
            return v.scalar_tensor_tensor(y, t, 1.5, y, ALU.add, ALU.mult)

        def rstd(v, total, y, t, step, base):
            for k in range(RSTD):
                if k:
                    v.wait_ge(step, base + k)
                rstd_step(v, k, total, y, t).then_inc(step, 1)
            v.wait_ge(step, base + RSTD)

        s_zero = sem("l0_zeros_ready")
        s_fin = sem("group_keys_ready")
        s_g = sem("group_bases_broadcast")
        s_w = sem("weights_loaded")
        s_i = sem("edges_loaded")
        s_x = sem("x_loaded")
        s_iota = sem("iota_ready")
        s_const = sem("constants_ready")
        s_dstep = sem("setup_vector_steps")
        s_bp = sem("bases_broadcast")
        s_wt = sem("worst_transposed")
        s_b2 = sem("b2_split")
        s_b2l = sem("b2_rest_ready")
        s_b2r = sem("b2_repeated")
        s_cen = sem("centred")
        s_sqd = sem("squared")
        s_norm = sem("normalised")
        s_pad = sem("pad_ready")
        s_padfree = sem("pad_free")
        s_tr = sem("transposed")
        s_cp = sem("columns_copied")
        s_cT = sem("columns_in_place")
        s_pr = sem("rows_multiplied")
        s_prc = sem("rows_copied")
        s_ps = sem("rows_stored")
        WL = 16 * 20

        with nc.Block() as block:
            @block.sync
            def _(sp):
                sp.dma_start(xs[:, :, :], x_t).then_inc(s_x, 16)
                sp.dma_start(dst_all[:, :, :], dst).then_inc(s_i, 16)
                sp.dma_start(src_all[:, :, :], src).then_inc(s_i, 16)
                sp.dma_start(src_d[:, :, :], src_dense).then_inc(s_i, 16)
                sp.dma_start(dst_d[:, :, :], dst_dense).then_inc(s_i, 16)
                sp.dma_start(w1n[F:2 * F, :], W1[0:F, :]).then_inc(s_w, 16)
                sp.dma_start(b1r[:, :], b1.unsqueeze(0)).then_inc(s_w, 16)
                sp.dma_start(wu[:, :], Wu).then_inc(s_w, 16)
                sp.dma_start(m1[:, :], M1).then_inc(s_w, 16)
                sp.dma_start(m2[:, :, :], M2.rearrange("(h p) f -> p h f", p=128)).then_inc(s_w, 16)
                for h in range(HS):
                    sp.dma_start(c1col[:, h:h + 1], c1[h * 128:(h + 1) * 128].unsqueeze(1)).then_inc(s_w, 16)
                for k in range(2):
                    sp.dma_start(gcol[k * F:(k + 1) * F, 0:1], g1.unsqueeze(1)).then_inc(s_w, 16)
                    sp.dma_start(gcol[k * F:(k + 1) * F, 1:2], be1.unsqueeze(1)).then_inc(s_w, 16)
                for k, row in enumerate((b2, bu, gn, bn, c2)):
                    sp.dma_start(rows[:, k, :], row.unsqueeze(0)).then_inc(s_w, 16)
                sp.wait_ge(s_const, 2)
                for k in range(2):
                    sp.dma_start(w2d[k * F:(k + 1) * F, k * F:(k + 1) * F], W2).then_inc(s_w, 16)
                    sp.dma_start(w1e[k * ED:(k + 1) * ED, k * F:(k + 1) * F], W1[F:F + ED, :]).then_inc(s_w, 16)
                sp.wait_ge(s_b2, 3)
                for k in range(3):
                    for c in range(BC):
                        sp.dma_start(b2rep[k:k + 1, c, :], b2part[:, k, :]).then_inc(s_b2r, 16)
                sp.wait_ge(s_b2r, 16 * 3 * BC)
                def chunk(g):
                    wait(sp, s_prc, BQ * g + BQ)
                    sp.dma_start(ptab_t[:, bass.ds(g * CH, CH), :], prow[:, :, :]).then_inc(s_ps, 16)
                repeated(sp, CHUNKS, chunk)
                sp.wait_ge(s_ps, 16 * CHUNKS)
                sp.wait_ge(s_i, 64)

            @block.gpsimd
            def _(pool):
                pool.iota(iot[:, :], [[1, 128]], base=0, channel_multiplier=-1).then_inc(s_iota, 1)
                pool.iota(wint[:, :, :], [[0, BC], [1, WIN]], base=0, channel_multiplier=0).then_inc(s_iota, 1)
                pool.iota(number_i[:, :], [[0, 1]], base=0, channel_multiplier=1).then_inc(s_iota, 1)
                pool.iota(key_i[:, :], [[1, max(PW * T, TP)]], base=0, channel_multiplier=0).then_inc(s_iota, 1)
                def chunk(g):
                    for q in range(BQ):
                        wait(pool, s_cp, BQ * g + q + 1)
                        pool.tensor_copy(cT[:, bass.ds(g * (CH * TP) + q * Q * TP, Q * TP)],
                                         cols[:, q % 2, :]).then_inc(s_cT, 1)
                repeated(pool, CHUNKS, chunk)

            @block.vector
            def _(v):
                v.memset(w2d[:, :], 0.0).then_inc(s_const, 1)
                v.memset(w1e[:, :], 0.0).then_inc(s_const, 1)
                v.memset(ones_b[:, :], 1.0).then_inc(s_const, 1)
                v.memset(ones[:, :], 1.0).then_inc(s_const, 1)
                v.memset(hpad[:, :, 0:F], 0.0).then_inc(s_const, 1)
                v.memset(cT[:, N:N + GW], 0.0).then_inc(s_const, 1)
                v.wait_ge(s_iota, 4)
                v.tensor_scalar(ident[:, :], iot[:, :], 0.0, None, ALU.is_equal).then_inc(s_const, 1)
                v.tensor_copy(winf[:, :, :], wint[:, :, :]).then_inc(s_const, 1)
                v.tensor_copy(keyf[:, :], key_i[:, 0:PW * T]).then_inc(s_const, 1)
                v.tensor_copy(lowf[:, :], key_i[:, 0:TP]).then_inc(s_const, 1)
                v.wait_ge(s_w, WL)
                for k, (lo, w) in enumerate(((F, w1n[F:2 * F, :]), (0, w1e[0:ED, 0:F]), (ED, w1e[ED:2 * ED, F:2 * F]),
                                             (0, b1r[:, :]))):
                    m = wmean[lo:lo + w.shape[0], k:k + 1]
                    v.tensor_reduce(m, w, X, ALU.add).then_inc(s_dstep, 1)
                    v.wait_ge(s_dstep, 3 * k + 1)
                    v.tensor_scalar(m, m, 1.0 / F, None, ALU.mult).then_inc(s_dstep, 1)
                    v.wait_ge(s_dstep, 3 * k + 2)
                    v.tensor_scalar(w, w, m, None, ALU.subtract).then_inc(s_dstep, 1)
                v.tensor_copy(b2part[:, 0, :], rows[:, 0, :]).then_inc(s_b2, 1)
                for k in range(2):
                    v.wait_ge(s_b2, k + 1)
                    if k:
                        v.wait_ge(s_b2l, k)
                    v.tensor_tensor(b2left[:, k, :], b2left[:, 0, :] if k else rows[:, 0, :], b2part[:, k, :],
                                    ALU.subtract).then_inc(s_b2l, 1)
                    v.wait_ge(s_b2l, k + 1)
                    v.tensor_copy(b2part[:, k + 1, :], b2left[:, k, :]).then_inc(s_b2, 1)
                v.wait_ge(s_x, 16)
                def chunk(g):
                    xg = xs[:, bass.ds(g * CH, CH), :]
                    v.tensor_reduce(stat[:, 0, :], xg, X, ALU.add).then_inc(s_norm, 1)
                    wait(v, s_norm, NORM * g + 1)
                    v.tensor_scalar(stat[:, 1, :], stat[:, 0, :], 1.0 / F, None, ALU.mult).then_inc(s_norm, 1)
                    wait(v, s_norm, NORM * g + 2)
                    wait(v, s_pad, g)
                    v.tensor_tensor(xc[:, :, :], xg, bcast(stat[:, 1, :], F), ALU.subtract).then_inc(s_cen, 1)
                    wait(v, s_sqd, g + 1)
                    v.tensor_reduce(stat[:, 2, :], sqc[:, :, :], X, ALU.add).then_inc(s_norm, 1)
                    wait(v, s_norm, NORM * g + 3)
                    rstd(v, stat[:, 2, :], stat[:, 3, :], stat[:, 0, :], s_norm, NORM * g + 3)
                    wait(v, s_cen, 2 * g + 1)
                    v.tensor_tensor(xc[:, :, :], xc[:, :, :], bcast(stat[:, 3, :], F), ALU.mult).then_inc(s_cen, 1)
                repeated(v, CHUNKS, chunk)
                v.wait_ge(s_i, 64)
                v.tensor_copy(base_int[:, :], dst_all[0:1, :, 0]).then_inc(s_dstep, 1)
                v.tensor_copy(base_row[:, :], dst_all[0:1, :, 0]).then_inc(s_dstep, 1)
                v.tensor_copy(pair_row[:, :, :], dst_d[0:1, :, 0:GC:2]).then_inc(s_dstep, 1)
                for k in range(BANKS):
                    lo, n = 512 * k, min(512, BLOCKS - 512 * k)
                    v.wait_ge(s_bp, k + 1)
                    v.tensor_copy(base_all[:, lo:lo + n], ag[k][:, 0:n]).then_inc(s_dstep, 1)
                v.wait_ge(s_dstep, 15 + BANKS)
                v.tensor_tensor(rel_all[:, :, :], dst_all[:, :, :], bcast(base_all[:, :], BC),
                                ALU.subtract).then_inc(s_dstep, 1)
                v.wait_ge(s_dstep, 16 + BANKS)
                for k in range(GBANKS):
                    lo, hi = k * PER, min((k + 1) * PER, DENSE)
                    v.wait_ge(s_g, k + 1)
                    first = mp[k][:, 0:(hi - lo) * GP].rearrange("p (s q) -> p s q", q=GP)
                    v.tensor_tensor(key_f[:, lo:hi, 0:GC:2], dst_d[:, lo:hi, 0:GC:2], first,
                                    ALU.subtract).then_inc(s_dstep, 1)
                    v.tensor_tensor(key_f[:, lo:hi, 1:GC:2], dst_d[:, lo:hi, 1:GC:2], first[:, :, 0:GC // 2],
                                    ALU.subtract).then_inc(s_dstep, 1)
                    v.tensor_tensor(offs[:, lo:hi, :], first,
                                    bcast(base_all[:, (G0 + lo) * UN:(G0 + hi) * UN:UN], GP),
                                    ALU.subtract).then_inc(s_dstep, 1)
                nb = 16 + BANKS + 3 * GBANKS
                v.wait_ge(s_dstep, nb)
                gaps = dst_d[:, :, 0:GP - 1].bitcast(f32)
                v.tensor_tensor(gaps, offs[:, :, 1:GP], offs[:, :, 0:GP - 1], ALU.subtract).then_inc(s_dstep, 1)
                v.wait_ge(s_dstep, nb + 1)
                tests = ((rel_all[:, :, :], ALU.max, 1.0, 1.0 - WIN), (rel_all[:, :, :], ALU.min, -1.0, 0.0),
                         (key_f[:, :, :], ALU.max, 1.0, 1.0 - PW), (key_f[:, :, :], ALU.min, -1.0, 0.0),
                         (offs[:, :, :], ALU.max, 1.0, float(PW - GW)), (gaps, ALU.max, 1.0, 1.0 - PW))
                for k, (t, op, _, _) in enumerate(tests):
                    v.tensor_reduce(worst[:, k:k + 1], t, XY, op).then_inc(s_dstep, 1)
                v.wait_ge(s_dstep, nb + 7)
                for k, (_, _, by, plus) in enumerate(tests):
                    v.tensor_scalar(worst[:, k:k + 1], worst[:, k:k + 1], by, plus, ALU.mult, ALU.add).then_inc(s_dstep, 1)
                v.wait_ge(s_dstep, nb + 13)
                v.tensor_reduce(worst[:, 6:7], worst[:, 0:6], X, ALU.max).then_inc(s_dstep, 1)
                v.tensor_scalar(low_f[:, :, :], src_d[:, :, :], 1.0 / TP, -(TP - 1) / 2 / TP,
                                ALU.mult, ALU.add).then_inc(s_dstep, 1)
                v.wait_ge(s_dstep, nb + 15)
                v.tensor_scalar(low_f[:, :, :], low_f[:, :, :], float(3 << 22), float(3 << 22),
                                ALU.add, ALU.subtract).then_inc(s_dstep, 1)
                v.wait_ge(s_dstep, nb + 16)
                v.scalar_tensor_tensor(key_f[:, :, :], key_f[:, :, :], float(T), low_f[:, :, :],
                                       ALU.mult, ALU.add).then_inc(s_dstep, 1)
                v.wait_ge(s_dstep, nb + 17)
                v.scalar_tensor_tensor(low_f[:, :, :], low_f[:, :, :], float(-TP), src_d[:, :, :],
                                       ALU.mult, ALU.add).then_inc(s_dstep, 1)
                v.wait_ge(s_dstep, nb + 18)
                v.tensor_copy(keys_all[:, 0:DENSE, 0:GC], key_f[:, :, :]).then_inc(s_fin, 1)
                v.tensor_copy(keys_all[:, 0:DENSE, GC:2 * GC], low_f[:, :, :]).then_inc(s_fin, 1)
                v.memset(keys_all[:, DENSE, :], 0.0).then_inc(s_fin, 1)
                v.tensor_scalar(at_int[:, :, :], offs[0:1, :, :], float(T), None, ALU.mult).then_inc(s_dstep, 1)
                v.tensor_copy(number[:, :], number_i[:, :]).then_inc(s_dstep, 1)
                v.wait_ge(s_dstep, nb + 20)
                v.wait_ge(s_wt, 1)
                v.tensor_scalar(held_all[:, :], offs[:, :, GP - 1], number[:, 0:1], float(PW),
                                ALU.subtract, ALU.add).then_inc(s_dstep, 1)
                v.wait_ge(s_dstep, nb + 21)
                v.tensor_scalar(held_all[:, :], held_all[:, :], 0.0, None, ALU.is_gt).then_inc(s_dstep, 1)
                v.tensor_reduce(worst_row[:, :], zp[0][0:1, 0:128], X, ALU.max).then_inc(s_dstep, 1)
                v.wait_ge(s_dstep, nb + 23)
                v.tensor_scalar(flag[:, :], worst_row[:, :], 0.0, None, ALU.is_gt).then_inc(s_dstep, 1)
                v.wait_ge(s_bp, BANKS + 1)
                v.tensor_copy(gb[:, :, :], zp[1][:, 0:2 * F].rearrange("p (k f) -> p k f", k=2)).then_inc(s_dstep, 1)

            @block.scalar
            def _(a):
                a.wait_ge(s_const, 10)
                def chunk(g):
                    wait(a, s_cen, 2 * g + 1)
                    a.activation(sqc[:, :, :], xc[:, :, :], ACT.Square).then_inc(s_sqd, 1)
                    wait(a, s_cen, 2 * g + 2)
                    wait(a, s_padfree, g + 1)
                    a.activation(hpad[:, :, F:2 * F], xc[:, :, :], ACT.Relu).then_inc(s_pad, 1)
                    for q in range(BQ):
                        wait(a, s_tr, BQ * g + q + 1)
                        wait(a, s_cT, BQ * g + max(q - 1, 0))
                        a.activation(cols[:, q % 2, :], tp[q % 2][:, 0:Q * TP], ACT.Copy).then_inc(s_cp, 1)
                        wait(a, s_pr, BQ * g + q + 1)
                        if q == 0:
                            wait(a, s_ps, 16 * g)
                        a.activation(prow[:, q * Q:(q + 1) * Q, :],
                                     mp[q % 2][0:TP, 0:Q * F].rearrange("p (t f) -> p t f", t=Q),
                                     ACT.Copy).then_inc(s_prc, 1)
                repeated(a, CHUNKS, chunk)

            @block.tensor
            def _(pe):
                pe.sem_inc(s_padfree, 1)
                pe.wait_ge(s_const, 10)
                pe.wait_ge(s_dstep, 12)
                def chunk(g):
                    wait(pe, s_pad, g + 1)
                    for q in range(BQ):
                        for t in range(Q):
                            mm = pe.transpose(tp[q % 2][:, t * TP:(t + 1) * TP], hpad[:, q * Q + t, :],
                                              ident[0:TP, 0:TP])
                        mm.then_inc(s_tr, 1)
                        wait(pe, s_cp, BQ * g + q + 1)
                        for t in range(Q):
                            o = mp[q % 2][0:TP, t * F:(t + 1) * F]
                            pe.matmul(o, ones[:, 0:TP], b1r[:, :], start=True, stop=False)
                            mm = pe.matmul(o, cols[F:2 * F, q % 2, t * TP:(t + 1) * TP],
                                           w1n[F:2 * F, :], start=False, stop=True)
                        mm.then_inc(s_pr, 1)
                        wait(pe, s_prc, BQ * g + q + 1)
                    pe.sem_inc(s_padfree, 1)
                repeated(pe, CHUNKS, chunk)
                pe.wait_ge(s_dstep, 15)
                for k in range(BANKS):
                    lo, n = 512 * k, min(512, BLOCKS - 512 * k)
                    pe.matmul(ag[k][:, 0:n], ones[:, :], base_row[:, lo:lo + n], start=True, stop=True).then_inc(s_bp, 1)
                for k in range(GBANKS):
                    lo, hi = k * PER, min((k + 1) * PER, DENSE)
                    pe.matmul(mp[k][:, 0:(hi - lo) * GP], ones[:, :],
                              pair_row[:, lo:hi, :].rearrange("o s q -> o (s q)"), start=True, stop=True).then_inc(s_g, 1)
                pe.matmul(zp[1][:, 0:2 * F], ones[:, :], rows[:, 2:4, :].rearrange("o k f -> o (k f)"),
                          start=True, stop=True).then_inc(s_bp, 1)
                pe.wait_ge(s_dstep, 16 + BANKS + 3 * GBANKS + 14)
                pe.transpose(zp[0][0:1, 0:128], worst[:, 6:7], ident[:, :]).then_inc(s_wt, 1)

        def gather(pool, table, n, j, done):
            for c in range(BC):
                pool.indirect_dma_start(
                    out=gat[:, j, c, :], out_offset=None, in_=table[:, :],
                    in_offset=bass.IndirectOffsetOnAxis(ap=idx[:, j, c:c + 1], axis=0)).then_inc(done, 16)

        def edge_products(pe, j):
            for k in range(PAIRS):
                two = 2 * k + 1 < BC
                mm = pe.matmul(zp[j % 2][:, 2 * k * F:(2 * k + 1 + two) * F],
                               ea[0:(1 + two) * ED, j, k * 128:(k + 1) * 128],
                               w1e[0:(1 + two) * ED, 0:(1 + two) * F], start=True, stop=True)
            return mm

        def transposes(pe, j):
            for k in range(PAIRS):
                mm = pe.transpose(tp[j % 2][:, k * 128:(k + 1) * 128],
                                  zn[:, j % 2, 2 * k:2 * k + 2, :].rearrange("p c f -> p (c f)"), ident[:, :])
            return mm

        def second_products(pe, j):
            o = mp[j % 2]
            pe.matmul(o[:, 0:BC * F], ones_b[:, :], b2rep[:, :, :].rearrange("o c f -> o (c f)"),
                      start=True, stop=False, skip_group_check=True)
            for k in range(BC // 2):
                mm = pe.matmul(o[:, k * 128:(k + 1) * 128], hT[:, j, k * 128:(k + 1) * 128], w2d[:, :],
                               start=False, stop=(k == PAIRS - 1), skip_group_check=True)
            if BC % 2:
                k = BC // 2
                mm = pe.matmul(o[:, k * 128:k * 128 + F], hT[0:F, j, k * 128:(k + 1) * 128],
                               w2d[0:F, 0:F], start=False, stop=True, skip_group_check=True)
            return mm

        def window_sums(pe, j, rows_of, to=ag):
            for c in range(BC):
                mm = pe.matmul(to[j % 2][0:F, 0:WIN], rows_of[:, c, :], oh[:, j, c, :],
                               start=(c == 0), stop=(c == BC - 1))
            return mm

        def one_hot(v, j, rel):
            return v.tensor_tensor(oh[:, j, :, :], winf[:, :, :], bcast(rel, WIN), ALU.is_equal)

        def block_of(t, n):
            return t[:, n, :] if isinstance(n, int) else t[:, bass.ds(n, 1), :].rearrange("p o c -> p (o c)")

        def load_edges(sp, n, j, done):
            def of(t):
                return t[n, :, :] if isinstance(n, int) else t[bass.ds(n, 1), :, :].rearrange("o k e -> (o k) e")
            sp.dma_start(ea[:, j, 0:(BC // 2) * 128], of(edge_pairs)).then_inc(done, 16)
            sp.dma_start(ea[0:ED, j, (BC // 2) * 128:], of(edge_last)).then_inc(done, 16)

        def indices(a, n, j):
            return a.activation(idx[:, j, :], block_of(src_all, n), ACT.Copy)

        def add_sums(v, n, j, of=ag):
            b = v.value_load(base_int[0:1, bass.ds(n, 1)], min_val=0, max_val=N)
            to = cT[0:F, bass.ds(b, WIN)]
            return v.tensor_tensor(to, to, of[j % 2][0:F, 0:WIN], ALU.add)

        def before(j):
            return 1 if j == 0 else 2

        def lagged(r, j, lag):
            r2, j2 = r + (j - lag) // UN, (j - lag) % UN
            return r2, j2, r2 * UN + j2

        def there(n):
            return not isinstance(n, int) or 0 <= n < BLOCKS

        def rounds(eng, step, lag, lead=1):
            for j in range(lead * UN):
                step(j // UN, j % UN)
            with eng.Fori(lead, ROUNDS - 1) as r:
                for j in range(UN):
                    step(r, j)
            for j in range(UN + lag):
                step(ROUNDS - 1, j)

        def flagged(eng):
            return eng.value_load(flag[0:1, 0:1], min_val=0, max_val=1)

        g_idx = sem("l0_index_ready")
        g_ea = [sem(f"l0_edges_loaded{j}") for j in range(UN)]
        g_gat = [sem(f"l0_rows_gathered{j}") for j in range(UN)]
        g_ep = sem("l0_edge_products")
        g_z = sem("l0_z_ready")
        g_sq = sem("l0_z_squared")
        g_red = sem("l0_squares_summed")
        g_ra = sem("l0_rstd_first_steps")
        g_rb = sem("l0_rstd_last_steps")
        g_n = sem("l0_z_normalised")
        g_t = sem("l0_z_transposed")
        g_h = sem("l0_hidden_ready")
        g_m = sem("l0_second_products")
        g_msg = sem("l0_messages_ready")
        g_oh = sem("l0_one_hot_ready")
        g_sum = sem("l0_window_summed")
        g_add = sem("l0_sums_added")

        with nc.Block() as block:
            @block.sync
            def _(sp):
                def step(r, j):
                    n = r * UN + j
                    wait(sp, g_ep, n - UN + 1)
                    load_edges(sp, n, j, g_ea[j])
                with sp.If(flagged(sp) == 0):
                    rounds(sp, step, 0)

            @block.gpsimd
            def _(pool):
                def step(r, j):
                    n = r * UN + j
                    wait(pool, g_idx, n + 1)
                    wait(pool, g_z, n - UN + 1)
                    wait_alone(pool, "gpsimd")
                    gather(pool, ptab, n, j, g_gat[j])
                with pool.If(flagged(pool) == 0):
                    rounds(pool, step, 0)

            @block.tensor
            def _(pe):
                def step(r, j):
                    _, s, n = lagged(r, j, 3)
                    if there(n):
                        wait(pe, g_n, n + 1)
                        wait(pe, g_h, n + 1 - before(s))
                        transposes(pe, s).then_inc(g_t, 1)
                    _, s, n = lagged(r, j, 4)
                    if there(n):
                        wait(pe, g_h, n + 1)
                        wait(pe, g_msg, n + 1 - before(s))
                        second_products(pe, s).then_inc(g_m, 1)
                    q, s, n = lagged(r, j, -1)
                    if there(n):
                        wait(pe, g_ea[s], q * 32 + 32)
                        wait(pe, g_z, n + 1 - before(s))
                        edge_products(pe, s).then_inc(g_ep, 1)
                    _, s, n = lagged(r, j, 5)
                    if there(n):
                        wait(pe, g_msg, n + 1)
                        wait(pe, g_oh, n + 1)
                        wait(pe, g_add, n + 1 - before(s))
                        window_sums(pe, s, msg[:, s, :, :]).then_inc(g_sum, 1)
                pe.wait_ge(s_zero, 1)
                with pe.If(flagged(pe) == 0):
                    pe.wait_ge(g_ea[0], 32)
                    edge_products(pe, 0).then_inc(g_ep, 1)
                    rounds(pe, step, 5, lead=2)

            @block.scalar
            def _(a):
                def step(r, j):
                    _, s, n = lagged(r, j, 0)
                    if there(n):
                        wait(a, g_z, n + 1)
                        wait(a, g_red, n + 1 - before(s))
                        a.activation(sq[:, s % 2, :, :], zb[:, s, :, :], ACT.Square).then_inc(g_sq, 1)
                        if there(n + UN):
                            indices(a, n + UN, s).then_inc(g_idx, 1)
                    _, s, n = lagged(r, j, 3)
                    if there(n):
                        wait(a, g_t, n + 1)
                        wait(a, g_m, n + 1 - UN)
                        a.activation(hT[:, s, :], tp[s % 2][:, 0:PAIRS * 128], ACT.Silu,
                                     bias=gcol[:, 1:2], scale=gcol[:, 0:1]).then_inc(g_h, 1)
                    _, s, n = lagged(r, j, 4)
                    if there(n):
                        wait(a, g_m, n + 1)
                        wait(a, g_sum, n + 1 - UN)
                        a.activation(msg[:, s, :, :], mp[s % 2][:, 0:BC * F].rearrange("p (c f) -> p c f", c=BC),
                                     ACT.Silu).then_inc(g_msg, 1)
                with a.If(flagged(a) == 0):
                    for j in range(UN):
                        indices(a, j, j).then_inc(g_idx, 1)
                    rounds(a, step, 4, lead=2)

            @block.vector
            def _(v):
                def first_step(k, s, n):
                    if there(n):
                        wait(v, g_ra if k else g_red, n * HALF + k if k else n + 1)
                        rstd_step(v, k, st[:, s, 0, :], st[:, s, 1, :], st[:, s, 2, :]).then_inc(g_ra, 1)

                def last_step(k, s, n):
                    if there(n):
                        wait(v, g_rb if k else g_ra, n * HALF + (k if k else HALF))
                        rstd_step(v, HALF + k, st[:, s, 0, :], st[:, s, 1, :], st[:, s, 2, :]).then_inc(g_rb, 1)

                def step(r, j):
                    q, s, n = lagged(r, j, 0)
                    _, s1, n1 = lagged(r, j, 1)
                    _, s2, n2 = lagged(r, j, 2)
                    _, s3, n3 = lagged(r, j, 3)
                    _, s6, n6 = lagged(r, j, 6)
                    last_step(0, s2, n2)
                    first_step(0, s1, n1)
                    if there(n):
                        wait(v, g_ep, n + 1)
                        wait(v, g_gat[s], q * (16 * BC) + 16 * BC)
                        wait(v, g_n, n + 1 - UN)
                        v.tensor_tensor(zb[:, s, :, :], zp[s % 2][:, 0:BC * F].rearrange("p (c f) -> p c f", c=BC),
                                        gat[:, s, :, :], ALU.add).then_inc(g_z, 1)
                    last_step(1, s2, n2)
                    first_step(1, s1, n1)
                    if there(n3):
                        wait(v, g_sum, n3 + 1 - UN)
                        one_hot(v, s3, block_of(rel_all, n3)).then_inc(g_oh, 1)
                    last_step(2, s2, n2)
                    first_step(2, s1, n1)
                    if there(n6):
                        wait(v, g_sum, n6 + 1)
                        wait(v, g_add, n6)
                        add_sums(v, n6, s6).then_inc(g_add, 1)
                    last_step(3, s2, n2)
                    first_step(3, s1, n1)
                    if there(n):
                        wait(v, g_sq, n + 1)
                        v.tensor_reduce(st[:, s, 0, :], sq[:, s % 2, :, :], X, ALU.add).then_inc(g_red, 1)
                    for k in range(4, HALF):
                        last_step(k, s2, n2)
                        first_step(k, s1, n1)
                    if there(n2):
                        wait(v, g_rb, n2 * HALF + HALF)
                        wait(v, g_t, n2 + 1 - before(s2))
                        v.tensor_tensor(zn[:, s2 % 2, 0:BC, :], zb[:, s2, :, :], bcast(st[:, s2, 1, :], F),
                                        ALU.mult).then_inc(g_n, 1)
                v.memset(zn[:, :, :, :], 0.0).then_inc(s_zero, 1)
                v.wait_ge(s_zero, 1)
                with v.If(flagged(v) == 0):
                    rounds(v, step, 6, lead=2)

        def general(layer, table):
            def gsem(name):
                return sem(f"general{layer}_{name}")
            x_done, x_idx, x_ea, x_gat, x_ep = map(gsem, ("block_done", "index_ready", "edges_loaded", "rows_gathered", "edge_products"))
            x_z, x_sq, x_st, x_n, x_t = map(gsem, ("z_ready", "squared", "rstd_steps", "normalised", "transposed"))
            x_h, x_m, x_msg, x_rel, x_oh = map(gsem, ("hidden_ready", "second_products", "messages_ready", "window_steps", "one_hot_ready"))
            x_sum, x_add = map(gsem, ("window_summed", "sums_added"))

            x_dst = gsem("dst_loaded")

            def sync(sp):
                with sp.Fori(0, BLOCKS) as n:
                    sp.wait_ge(x_done, n + 1)
                    sp.dma_start(dst_n[:, :], block_of(dst, n)).then_inc(x_dst, 16)
                    if layer == 0:
                        load_edges(sp, n, 0, x_ea)

            def gpsimd(pool):
                with pool.Fori(0, BLOCKS) as n:
                    pool.wait_ge(x_idx, n + 1)
                    wait_alone(pool, "gpsimd")
                    gather(pool, table, n, 0, x_gat)

            def scalar(a):
                with a.Fori(0, BLOCKS) as n:
                    a.wait_ge(x_done, n + 1)
                    indices(a, n, 0).then_inc(x_idx, 1)
                    if layer == 0:
                        a.wait_ge(x_z, n + 1)
                        a.activation(sq[:, 0, :, :], gat[:, 0, :, :], ACT.Square).then_inc(x_sq, 1)
                        a.wait_ge(x_t, n + 1)
                        a.activation(hT[:, 0, :], tp[0][:, 0:PAIRS * 128], ACT.Silu,
                                     bias=gcol[:, 1:2], scale=gcol[:, 0:1]).then_inc(x_h, 1)
                        a.wait_ge(x_m, n + 1)
                        a.activation(msg[:, 0, :, :], mp[0][:, 0:BC * F].rearrange("p (c f) -> p c f", c=BC),
                                     ACT.Silu).then_inc(x_msg, 1)

            def tensor(pe):
                with pe.Fori(0, BLOCKS) as n:
                    if layer == 0:
                        pe.wait_ge(x_ea, 32 * n + 32)
                        pe.wait_ge(x_done, n + 1)
                        edge_products(pe, 0).then_inc(x_ep, 1)
                        pe.wait_ge(x_n, n + 1)
                        transposes(pe, 0).then_inc(x_t, 1)
                        pe.wait_ge(x_h, n + 1)
                        second_products(pe, 0).then_inc(x_m, 1)
                        pe.wait_ge(x_msg, n + 1)
                    else:
                        pe.wait_ge(x_gat, n * (16 * BC) + 16 * BC)
                    wait_alone(pe, "tensor")
                    with pe.Fori(0, WINDOWS) as w:
                        k = n * WINDOWS + w
                        pe.wait_ge(x_oh, k + 1)
                        pe.wait_ge(x_add, k + 1)
                        window_sums(pe, 0, msg[:, 0, :, :] if layer == 0 else gat[:, 0, :, :]).then_inc(x_sum, 1)

            def vector(v):
                v.sem_inc(x_done, 1)
                v.sem_inc(x_sum, 1)
                v.sem_inc(x_add, 1)
                with v.Fori(0, BLOCKS) as n:
                    v.wait_ge(x_dst, 16 * n + 16)
                    v.memset(wbase[:, :], 0.0).then_inc(x_rel, 1)
                    if layer == 0:
                        v.wait_ge(x_ep, n + 1)
                        v.wait_ge(x_gat, n * (16 * BC) + 16 * BC)
                        z = gat[:, 0, :, :]
                        v.tensor_tensor(z, zp[0][:, 0:BC * F].rearrange("p (c f) -> p c f", c=BC), z,
                                        ALU.add).then_inc(x_z, 1)
                        v.wait_ge(x_sq, n + 1)
                        v.tensor_reduce(st[:, 0, 0, :], sq[:, 0, :, :], X, ALU.add).then_inc(x_st, 1)
                        v.wait_ge(x_st, n * (RSTD + 1) + 1)
                        rstd(v, st[:, 0, 0, :], st[:, 0, 1, :], st[:, 0, 2, :], x_st, n * (RSTD + 1) + 1)
                        v.tensor_tensor(zn[:, 0, 0:BC, :], z, bcast(st[:, 0, 1, :], F), ALU.mult).then_inc(x_n, 1)
                    with v.Fori(0, WINDOWS) as w:
                        k = n * WINDOWS + w
                        v.wait_ge(x_rel, k * 2 + n + 1)
                        v.tensor_scalar(reln[:, :], dst_n[:, :], wbase[:, :], None, ALU.subtract).then_inc(x_rel, 1)
                        v.wait_ge(x_rel, k * 2 + n + 2)
                        v.wait_ge(x_sum, k + 1)
                        one_hot(v, 0, reln[:, :]).then_inc(x_oh, 1)
                        v.tensor_scalar(wbase[:, :], wbase[:, :], float(WIN), None, ALU.add).then_inc(x_rel, 1)
                        v.wait_ge(x_sum, k + 2)
                        v.wait_ge(x_add, k + 1)
                        to = cT[0:F, bass.ds(w * WIN, WIN)]
                        v.tensor_tensor(to, to, ag[0][0:F, 0:WIN], ALU.add).then_inc(x_add, 1)
                    v.wait_ge(x_add, n * WINDOWS + WINDOWS + 1)
                    v.wait_ge(x_oh, n * WINDOWS + WINDOWS)
                    v.sem_inc(x_done, 1)

            with nc.Block() as block:
                @block.sync
                def _(sp):
                    with sp.If(flagged(sp) != 0):
                        sync(sp)

                @block.gpsimd
                def _(pool):
                    with pool.If(flagged(pool) != 0):
                        gpsimd(pool)

                @block.tensor
                def _(pe):
                    with pe.If(flagged(pe) != 0):
                        tensor(pe)

                @block.scalar
                def _(a):
                    with a.If(flagged(a) != 0):
                        scalar(a)

                @block.vector
                def _(v):
                    with v.If(flagged(v) != 0):
                        vector(v)

        general(0, ptab)

        u_w = sem("update_columns_ready")
        u_u = sem("update_products")
        u_s = sem("update_ready")
        u_v = sem("update_vector_steps")
        u_c = sem("update_centred")
        u_q = sem("update_squared")
        u_h = sem("layer1_h_ready")
        u_hi = sem("h_high_part")
        u_left = sem("h_rest")
        u_mid = sem("h_middle_part")
        u_low = sem("h_low_part")
        u_st = sem("layer1_rows_stored")
        u_t = sem("layer1_transposed")
        u_cp = sem("layer1_columns_copied")

        with nc.Block() as block:
            @block.gpsimd
            def _(pool):
                def chunk(g):
                    for q in range(BQ):
                        wait(pool, u_u, BQ * g + max(q - 1, 0))
                        pool.tensor_copy(cols[:, q % 2, :],
                                         cT[:, bass.ds(g * (CH * TP) + q * Q * TP, Q * TP)]).then_inc(u_w, 1)
                repeated(pool, CHUNKS, chunk)

            @block.tensor
            def _(pe):
                def chunk(g):
                    for q in range(BQ):
                        wait(pe, u_w, BQ * g + q + 1)
                        wait(pe, u_s, BQ * g + max(q - 1, 0))
                        for t in range(Q):
                            o = mp[q % 2][0:TP, t * F:(t + 1) * F]
                            pe.matmul(o, ones[:, 0:TP], rows[:, 1, :], start=True, stop=False)
                            mm = pe.matmul(o, cols[:, q % 2, t * TP:(t + 1) * TP], wu[:, :],
                                           start=False, stop=True)
                        mm.then_inc(u_u, 1)
                    wait(pe, u_h, g + 1)
                    for q in range(BQ):
                        wait(pe, u_cp, BQ * g + max(q - 1, 0))
                        wait_alone(pe, "tensor")
                        for t in range(Q):
                            mm = pe.transpose(tp[q % 2][0:F, t * TP:(t + 1) * TP], prow[:, q * Q + t, :],
                                              ident[0:TP, 0:TP])
                        mm.then_inc(u_t, 1)
                repeated(pe, CHUNKS, chunk)

            @block.scalar
            def _(a):
                def chunk(g):
                    for q in range(BQ):
                        wait(a, u_u, BQ * g + q + 1)
                        wait(a, u_v, g * (2 * NORM + 2))
                        a.activation(xc[:, q * Q:(q + 1) * Q, :],
                                     mp[q % 2][0:TP, 0:Q * F].rearrange("p (t f) -> p t f", t=Q),
                                     ACT.Silu).then_inc(u_s, 1)
                    for k in range(2):
                        wait(a, u_c, 2 * g + k + 1)
                        wait(a, u_low, g)
                        a.activation(sqc[:, :, :], xc[:, :, :], ACT.Square).then_inc(u_q, 1)
                    wait(a, u_v, g * (2 * NORM + 2) + 2 * NORM + 2)
                    wait(a, u_st, 16 * g)
                    wait(a, u_t, BQ * g)
                    wait(a, u_low, g)
                    a.activation(prow[:, :, :], xc[:, :, :], ACT.Relu).then_inc(u_h, 1)
                    part = hparts[:, bass.ds(g * CH, CH), :, :]
                    wait(a, u_h, g + 1)
                    a.activation(part[:, :, 0, :], prow[:, :, :], ACT.Copy).then_inc(u_hi, 1)
                    wait(a, u_left, g + 1)
                    a.activation(part[:, :, 1, :], sqc[:, :, :], ACT.Copy).then_inc(u_mid, 1)
                    for q in range(BQ):
                        wait(a, u_t, BQ * g + q + 1)
                        a.activation(cT[0:F, bass.ds(g * (CH * TP) + q * Q * TP, Q * TP)],
                                     tp[q % 2][0:F, 0:Q * TP], ACT.Copy).then_inc(u_cp, 1)
                repeated(a, CHUNKS, chunk)

            @block.vector
            def _(v):
                def norm(base, g, k):
                    v.tensor_reduce(stat[:, 0, :], xc[:, :, :], X, ALU.add).then_inc(u_v, 1)
                    v.wait_ge(u_v, base + 1)
                    v.tensor_scalar(stat[:, 1, :], stat[:, 0, :], 1.0 / F, None, ALU.mult).then_inc(u_v, 1)
                    v.wait_ge(u_v, base + 2)
                    v.tensor_tensor(xc[:, :, :], xc[:, :, :], bcast(stat[:, 1, :], F), ALU.subtract).then_inc(u_c, 1)
                    v.wait_ge(u_q, 2 * g + k + 1)
                    v.tensor_reduce(stat[:, 2, :], sqc[:, :, :], X, ALU.add).then_inc(u_v, 1)
                    v.wait_ge(u_v, base + 3)
                    rstd(v, stat[:, 2, :], stat[:, 3, :], stat[:, 0, :], u_v, base + 3)
                    v.wait_ge(u_c, 2 * g + k + 1)
                    v.tensor_tensor(xc[:, :, :], xc[:, :, :], bcast(stat[:, 3, :], F), ALU.mult).then_inc(u_v, 1)

                u_x = sem("residual_steps")
                def chunk(g):
                    wait(v, u_s, BQ * g + BQ)
                    norm(g * (2 * NORM + 2), g, 0)
                    wait(v, u_v, g * (2 * NORM + 2) + NORM + 1)
                    v.tensor_tensor(xc[:, :, :], xc[:, :, :], per_tile(gb[0:TP, 0, :], CH), ALU.mult).then_inc(u_x, 1)
                    wait(v, u_x, 4 * g + 1)
                    v.tensor_tensor(xc[:, :, :], xc[:, :, :], per_tile(gb[0:TP, 1, :], CH), ALU.add).then_inc(u_x, 1)
                    wait(v, u_x, 4 * g + 2)
                    xg = xs[:, bass.ds(g * CH, CH), :]
                    v.tensor_tensor(xc[:, :, :], xg, xc[:, :, :], ALU.add).then_inc(u_x, 1)
                    wait(v, u_x, 4 * g + 3)
                    v.tensor_scalar(xg, xc[:, :, :], 1.0, None, ALU.mult).then_inc(u_x, 1)
                    wait(v, u_x, 4 * g + 4)
                    norm(g * (2 * NORM + 2) + NORM + 1, g, 1)
                    part = hparts[:, bass.ds(g * CH, CH), :, :]
                    wait(v, u_hi, g + 1)
                    v.tensor_tensor(sqc[:, :, :], prow[:, :, :], part[:, :, 0, :], ALU.subtract).then_inc(u_left, 1)
                    wait(v, u_mid, g + 1)
                    wait(v, u_left, g + 1)
                    v.tensor_tensor(part[:, :, 2, :], sqc[:, :, :], part[:, :, 1, :], ALU.subtract).then_inc(u_low, 1)
                repeated(v, CHUNKS, chunk)

            @block.sync
            def _(sp):
                def chunk(g):
                    wait(sp, u_h, g + 1)
                    sp.dma_start(htab_t[:, bass.ds(g * CH, CH), :], prow[:, :, :]).then_inc(u_st, 16)
                repeated(sp, CHUNKS, chunk)
                sp.wait_ge(u_st, 16 * CHUNKS)

        k_idx = sem("l1_index_ready")
        k_gat = [sem(f"l1_rows_gathered{j}") for j in range(UN)]
        k_oh = sem("l1_one_hot_ready")
        k_sum = sem("l1_window_summed")
        k_add = sem("l1_sums_added")
        d_zero = sem("counts_zeroed")
        d_load = sem("group_keys_loaded")
        d_half = sem("column_keys_compared")
        d_key = sem("column_one_hots_ready")
        d_use = sem("columns_multiplied")
        d_first = sem("pair_first_node_added")
        d_copy = sem("pair_nodes_copied")
        d_sum = sem("group_summed")
        d_raw = sem("group_sums_copied")
        d_turn = sem("group_sums_turned")
        d_add = sem("group_sums_added")
        WT = PW // 3 * T
        built = [ps[:TP, 3 * k:3 * k + 3, 0:WT] for k in range(2)]
        wide = ps[:, 6, 0:3 * F]
        turned = ps[0:F, 6, 3 * F:3 * F + GW]
        agl = [ps[:, 7, :]] * 2

        def columns_back(c):
            return OHS if c >= OHS else c + GC - max(k for k in range(GC) if k % OHS == c)

        def group_of(t, d):
            return t[:, d, :] if isinstance(d, int) else t[:, bass.ds(d, 1), :].rearrange("p o c -> p (o c)")

        with nc.Block() as block:
            @block.gpsimd
            def _(pool):
                def step(r, j):
                    n = r * UN + j
                    wait(pool, k_idx, n + 1)
                    wait(pool, k_sum, n - UN + 1)
                    wait_alone(pool, "gpsimd")
                    gather(pool, htab, n, j, k_gat[j])

                def both(r):
                    for j in range(UN):
                        step(r, j)
                with pool.If(flagged(pool) == 0):
                    repeated(pool, G0, both)

            @block.scalar
            def _(a):
                def index(r, j):
                    n = r * UN + j
                    wait(a, k_sum, n - UN + 1)
                    indices(a, n, j).then_inc(k_idx, 1)

                def both(d):
                    for q in range(GP):
                        wait(a, d_use, d * GC + min(2 * q + 2, GC))
                        if q == 0:
                            wait(a, d_sum, d)
                        wait(a, d_copy, (d * GP + q) * 2)
                        at = a.value_load(group_of(at_int, d)[:, q:q + 1], min_val=0, max_val=GW * T)
                        a.activation(cnt[:, bass.ds(at + WT, 2 * WT)].rearrange("p (b k) -> p b k", b=2),
                                     built[q % 2][:, 1:3, :], ACT.Copy).then_inc(d_copy, 1)
                        wait(a, d_first, d * GP + q + 1)
                        a.activation(cnt[:, bass.ds(at + T, WT - T)], built[q % 2][:, 0, T:WT], ACT.Copy).then_inc(d_copy, 1)
                        if q % 2 == 1 and q < 2 * UN:
                            index(d + 1, q // 2)
                    wait(a, d_sum, d + 1)
                    wait(a, d_turn, d)
                    held = held_all[:, d:d + 1] if isinstance(d, int) else held_all[:, bass.ds(d, 1)]
                    a.activation(raw[:, :], wide, ACT.Copy, scale=held).then_inc(d_raw, 1)
                with a.If(flagged(a) == 0):
                    for j in range(UN):
                        index(0, j)
                    a.wait_ge(d_zero, 1)
                    repeated(a, DENSE, both)

            @block.tensor
            def _(pe):
                def sums(r, j):
                    n = r * UN + j
                    wait(pe, k_gat[j], r * (16 * BC) + 16 * BC)
                    wait(pe, k_oh, n + 1)
                    wait(pe, k_add, n)
                    window_sums(pe, j, gat[:, j, :, :], agl).then_inc(k_sum, 1)

                def turn(d):
                    wait(pe, d_raw, d + 1)
                    wait(pe, d_add, d)
                    for k in range(3):
                        mm = pe.matmul(turned, raw[:, k * F:(k + 1) * F], ident[:, :], start=(k == 0), stop=(k == 2))
                    mm.then_inc(d_turn, 1)

                def both(d):
                    for q in range(GP):
                        back = 2 if q > 1 else 1 if q == 0 else 3
                        wait(pe, d_first, d * GP + q + 1 - back)
                        wait(pe, d_copy, (d * GP + q + 1 - back) * 2)
                        for c in range(2 * q, min(2 * q + 2, GC)):
                            wait(pe, d_key, d * GC + c + 1)
                            for b in range(3):
                                mm = pe.matmul(built[q % 2][:, b, :], ohl[:, c % OHS, 0:TP],
                                               ohk[:, c % OHS, b * WT:(b + 1) * WT],
                                               start=(c == 2 * q), stop=(c == min(2 * q + 1, GC - 1)))
                            mm.then_inc(d_use, 1)
                        if q % 2 == 1 and q < 2 * UN:
                            sums(d, q // 2)
                        if q == 2 and not (isinstance(d, int) and d == 0):
                            turn(d - 1)
                    wait(pe, d_first, d * GP + GP)
                    wait(pe, d_copy, (d * GP + GP) * 2)
                    wait(pe, d_raw, d)
                    wait(pe, d_add, d)
                    for t in range(T):
                        mm = pe.matmul(wide, cnt[:, t:t + (GW - 1) * T + 1:T],
                                       hparts[:, t, :, :].rearrange("p k f -> p (k f)"), start=(t == 0), stop=(t == T - 1))
                    mm.then_inc(d_sum, 1)
                with pe.If(flagged(pe) == 0):
                    repeated(pe, DENSE, both)
                    turn(DENSE - 1)
                    for j in range(UN):
                        sums(DENSE, j)

            @block.vector
            def _(v):
                def one_hots(r, j):
                    n = r * UN + j
                    wait(v, k_sum, n + 1 - UN)
                    one_hot(v, j, block_of(rel_all, n)).then_inc(k_oh, 1)

                def add_block(r, j, groups):
                    n = r * UN + j
                    wait(v, k_sum, n + 1)
                    wait(v, k_add, n)
                    wait(v, d_add, groups)
                    add_sums(v, n, j, agl).then_inc(k_add, 1)

                def add_group(d, blocks):
                    base = v.value_load(base_int[0:1, bass.ds((d + G0) * UN, 1)], min_val=0, max_val=N)
                    wait(v, d_turn, d + 1)
                    wait(v, k_add, blocks)
                    wait(v, d_add, d)
                    to = cT[0:F, bass.ds(base, GW)]
                    v.tensor_tensor(to, to, turned, ALU.add).then_inc(d_add, 1)

                def add_first(d, q):
                    y = d * GP + q
                    if q == 0:
                        wait(v, d_use, d * GC + 2)
                        wait(v, d_sum, d)
                        v.tensor_copy(cnt[:, 0:T], built[0][:, 0, 0:T]).then_inc(d_first, 1)
                        return
                    at = v.value_load(group_of(at_int, d)[:, q:q + 1], min_val=0, max_val=GW * T)
                    wait(v, d_use, d * GC + min(2 * q + 2, GC))
                    wait(v, d_copy, y * 2)
                    wait(v, d_first, y)
                    to = cnt[:, bass.ds(at, T)]
                    v.tensor_tensor(to, to, built[q % 2][:, 0, 0:T], ALU.add).then_inc(d_first, 1)

                def load_keys(d):
                    wait_alone(v, "vector")
                    v.tensor_copy(keys[:, :], group_of(keys_all, d)).then_inc(d_load, 1)

                def both(d):
                    wait(v, d_load, d + 1)
                    for c in range(GC):
                        wait(v, d_use, d * GC + c + 1 - columns_back(c))
                        v.tensor_scalar(ohk[:, c % OHS, :], keyf[:, :], keys[:, c:c + 1], None, ALU.is_equal)\
                         .then_inc(d_half, 1)
                        v.tensor_scalar(ohl[:, c % OHS, 0:TP], lowf[:, :], keys[:, GC + c:GC + c + 1], None, ALU.is_equal)\
                         .then_inc(d_key, 1)
                        if c % 2 == 1 and c > 1:
                            add_first(d, c // 2 - 1)
                        if c % 4 == 2 and c // 4 < UN - 1:
                            one_hots(d, c // 4 + 1)
                        if c % 4 == 2 and c >= 6:
                            add_block(d, c // 4 - 1, d - (c < 12))
                        if c == 12 and not (isinstance(d, int) and d == 0):
                            add_group(d - 1, d * UN + 2)
                    wait(v, d_key, d * GC + GC)
                    load_keys(d + 1)
                    add_first(d, GP - 2)
                    add_first(d, GP - 1)
                    one_hots(d + 1, 0)
                with v.If(flagged(v) == 0):
                    v.memset(cnt[:, :], 0.0).then_inc(d_zero, 1)
                    v.wait_ge(s_fin, 3)
                    load_keys(0)
                    v.wait_ge(d_zero, 1)
                    one_hots(0, 0)
                    repeated(v, DENSE, both)
                    add_group(DENSE - 1, DENSE * UN)
                    for j in range(UN):
                        if j:
                            one_hots(DENSE, j)
                        add_block(DENSE, j, DENSE)

        general(1, htab)

        e_h = sem("mlp_hidden_products")
        e_r = sem("mlp_hidden_ready")
        e_o = sem("mlp_products")
        e_x = sem("result_ready")
        e_st = sem("result_stored")
        BATCHES = T // Q

        with nc.Block() as block:
            @block.tensor
            def _(pe):
                def batch(b):
                    wait(pe, e_r, HS * b)
                    for h in range(HS):
                        pe.matmul(tp[h][:, 0:Q * TP], m1[:, h * 128:(h + 1) * 128],
                                  cT[0:F, bass.ds(b * (Q * TP), Q * TP)], start=True, stop=True).then_inc(e_h, 1)
                    wait(pe, e_r, HS * b + HS)
                    wait(pe, e_x, b)
                    for t in range(Q):
                        o = mp[0][0:TP, t * F:(t + 1) * F]
                        pe.matmul(o, ones[:, 0:TP], rows[:, 4, :], start=True, stop=False)
                        for h in range(HS):
                            mm = pe.matmul(o, hid[:, h, t * TP:(t + 1) * TP], m2[:, h, :],
                                           start=False, stop=(h == HS - 1))
                    mm.then_inc(e_o, 1)
                repeated(pe, BATCHES, batch)

            @block.scalar
            def _(a):
                def batch(b):
                    for h in range(HS):
                        wait(a, e_h, HS * b + h + 1)
                        wait(a, e_o, b)
                        a.activation(hid[:, h, :], tp[h][:, 0:Q * TP], ACT.Relu, bias=c1col[:, h:h + 1]).then_inc(e_r, 1)
                repeated(a, BATCHES, batch)

            @block.vector
            def _(v):
                def batch(b):
                    wait(v, e_o, b + 1)
                    xb = xs[:, bass.ds(b * Q, Q), :]
                    v.tensor_tensor(xb, xb, mp[0][0:TP, 0:Q * F].rearrange("p (t f) -> p t f", t=Q),
                                    ALU.add).then_inc(e_x, 1)
                repeated(v, BATCHES, batch)

            @block.sync
            def _(sp):
                def batch(b):
                    wait(sp, e_x, b + 1)
                    sp.dma_start(out_t[:, bass.ds(b * Q, Q), :], xs[:, bass.ds(b * Q, Q), :]).then_inc(e_st, 16)
                repeated(sp, BATCHES, batch)
                sp.wait_ge(e_st, 16 * BATCHES)


BLOCK_COLUMNS = 5
INPUTS = ["x", "src", "dst", "src_dense", "dst_dense", "edge_pairs", "edge_last", "L0_gnn_W1", "L0_gnn_b1", "L0_gnn_g1", "L0_gnn_be1", "L0_gnn_W2", "L0_gnn_b2",
          "L0_gnn_Wu", "L0_gnn_bu", "L0_gnn_gn", "L0_gnn_bn", "L1_gnn_W1", "L1_gnn_b1", "L1_gnn_W2", "L1_gnn_b2"]


def kernel(x, src, dst, edge_attr_32, **weights):
    import numpy as np
    import concourse.bacc as bacc
    from concourse.bass_utils import run_bass_kernel_spmd

    E, ED = edge_attr_32.shape
    edges = 128 * BLOCK_COLUMNS
    blocks = E // edges
    rounds, columns = blocks // 5, 5 * BLOCK_COLUMNS
    arrays = {"x": np.ascontiguousarray(x)}
    for name, a in (("src", src), ("dst", dst)):
        arrays[name] = np.ascontiguousarray(np.asarray(a).reshape(blocks, 128, BLOCK_COLUMNS).transpose(1, 0, 2))
        arrays[name + "_dense"] = np.ascontiguousarray(
            np.asarray(a).reshape(rounds, columns, 128)[(rounds + 1) // 2:].transpose(2, 0, 1))
    ea = np.asarray(edge_attr_32).reshape(blocks, 128, BLOCK_COLUMNS, ED)
    pairs = BLOCK_COLUMNS // 2
    arrays["edge_pairs"] = np.ascontiguousarray(
        ea[:, :, :2 * pairs].reshape(blocks, 128, pairs, 2, ED).transpose(0, 3, 4, 2, 1)
        .reshape(blocks, 2 * ED, pairs * 128))
    arrays["edge_last"] = np.ascontiguousarray(ea[:, :, 2 * pairs].transpose(0, 2, 1))
    for name, a in weights.items():
        arrays[name] = np.ascontiguousarray(a)

    nc = bacc.Bacc("TRN2", target_bir_lowering=False, num_devices=1)
    args = [nc.dram_tensor(f"in_{n}", arrays[n].shape, mybir.dt.from_np(arrays[n].dtype), kind="ExternalInput").ap()
            for n in INPUTS]
    out = nc.dram_tensor("out", arrays["x"].shape, mybir.dt.float32, kind="ExternalOutput").ap()
    build_gnn(nc, *args, out)
    r = run_bass_kernel_spmd(nc, [{f"in_{n}": arrays[n] for n in INPUTS}], core_ids=[0])
    return r.results[0]["out"]
```

```python
import concourse.bass as bass
from concourse import mybir
from contextlib import ExitStack


def build_gnn(nc, x, src, dst, src_dense, dst_dense, edge_pairs, edge_last, W1, b1, g1, be1, W2, b2, Wu, bu, gn, bn, M1, c1, M2, c2, out):
    f32, bf16, f16, i32 = mybir.dt.float32, mybir.dt.bfloat16, mybir.dt.float16, mybir.dt.int32
    ALU = mybir.AluOpType
    ACT = mybir.ActivationFunctionType
    X = mybir.AxisListType.X
    XY = mybir.AxisListType.XY
    EPS = 1e-5

    N, F = x.shape
    ED = edge_last.shape[1]
    BLOCKS, BC = src.shape[1], src.shape[2]
    EB = 128 * BC
    UN = 5
    ROUNDS = BLOCKS // UN
    WIN = 64
    WINDOWS = -(-N // WIN)
    H = M1.shape[1]
    HS = H // 128
    TP = max(t for t in range(1, 129) if N % t == 0)
    T = N // TP
    Q = 4
    CH = 20 if T % 20 == 0 else Q
    CHUNKS = T // CH
    BQ = CH // Q
    PAIRS = -(-BC // 2)
    DENSE, GC = src_dense.shape[1], src_dense.shape[2]
    GP = -(-GC // 2)
    PW = 12
    GW = 128
    BANKS = -(-BLOCKS // 512)
    PER = 512 // GP
    GBANKS = -(-DENSE // PER)
    G0 = ROUNDS - DENSE
    assert GC == UN * BC and G0 == DENSE + 1 and 4 * T <= 512 and PW == 12 and DENSE % 2 == 0
    assert BC % 2 == 1 and BLOCKS % UN == 0 and T % CH == 0 and CH % Q == 0 and F == 64 and ED == 32 and TP * Q <= 512

    ctx = ExitStack()
    with ctx:
        def sb(name, shape, dt=f32):
            return ctx.enter_context(nc.sbuf_tensor(name, shape, dt))

        def region(name, size):
            left = [sb(name, [128, size // 4]), 0]

            def view(shape, dt=f32):
                count = 1
                for n in shape[1:]:
                    count *= n
                words = (count * (2 if dt in (bf16, f16) else 4) + 3) // 4
                part = left[0][0:shape[0], left[1]:left[1] + words]
                left[1] += words
                assert left[1] <= size // 4, (name, left[1] * 4, size)
                if dt != f32:
                    part = part.bitcast(dt)[:, 0:count]
                if len(shape) > 2:
                    names = "abcd"[:len(shape) - 1]
                    part = part.rearrange(f"p ({' '.join(names)}) -> p {' '.join(names)}",
                                          **{k: n for k, n in zip(names[:-1], shape[1:-1])})
                return part

            def again(keep=0):
                left[1] = keep // 4
            return view, again

        def sem(name):
            return ctx.enter_context(nc.semaphore(name))

        ptab = nc.dram_tensor("layer0_rows", (N, F), f32, kind="Internal").ap()
        htab = nc.dram_tensor("layer1_rows", (N, F), f32, kind="Internal").ap()
        xtab = nc.dram_tensor("residual_rows", (N, F), f32, kind="Internal").ap()

        cT = sb("cT", [128, N + GW])
        src_all = sb("src_all", [128, BLOCKS, BC], i32)
        rel_all = sb("rel_all", [128, BLOCKS, BC], bf16)
        base_int = sb("base_int", [1, BLOCKS], i32)
        flag = sb("flag", [1, 1], i32)
        worst = sb("worst", [128, 8])
        worst_row = sb("worst_row", [1, 1])
        number_i = sb("number_i", [128, 1], i32)
        number = sb("number", [128, 1])
        keys_all = sb("keys_all", [128, DENSE + 1, 2 * GC], f16)
        keys = sb("keys", [128, 2 * GC])
        held_all = sb("held_all", [128, DENSE])
        at_int = sb("at_int", [1, DENSE, GP], i32)

        w1n = sb("w1n", [128, F])
        w1e = sb("w1e", [2 * ED, 2 * F])
        b1r = sb("b1r", [1, F])
        wmean = sb("wmean", [128, 4])
        w2d = sb("w2d", [128, 128])
        wu = sb("wu", [128, F])
        m1 = sb("m1", [F, H])
        m2 = sb("m2", [128, HS, F])
        gcol = sb("gcol", [128, 2])
        c1col = sb("c1col", [128, HS])
        rows = sb("rows", [1, 5, F])
        b2rep = sb("b2rep", [3, BC, F], bf16)
        ones_b = sb("ones_b", [3, 128], bf16)
        gb = sb("gb", [128, 3, F])
        ones = sb("ones", [1, 128])
        ident = sb("ident", [128, 128])
        winf = sb("winf", [128, BC, WIN], bf16)
        keyf = sb("keyf", [128, PW * T], f16)
        lowf = sb("lowf", [128, TP], f16)
        wbase = sb("wbase", [128, 1])
        reln = sb("reln", [128, BC])
        dst_n = sb("dst_n", [128, BC], i32)
        stat = sb("stat", [TP, 4, CH])

        idx = sb("idx", [128, UN, BC], i32)
        gat = sb("gat", [128, UN, BC, F])
        oh = sb("oh", [128, UN, BC, WIN])
        st = sb("st", [128, UN, 3, BC])

        OHS = 4
        XB = T * F * 4
        view, again = region("node_buffers", max(XB + 5 * CH * F * 4 + 2 * Q * TP * 4, XB + 3 * HS * Q * TP * 4,
                                                 2 * (GW + PW) * T * 2 + 3 * F * 4 + OHS * (PW * T + 128) * 2))
        xs = view([TP, T, F])
        xc = view([TP, CH, F])
        sqc = view([TP, CH, F])
        prow = view([TP, CH, F])
        cols = view([128, 2, Q * TP])
        hpad = view([TP, CH, 2 * F])
        b1q = view([1, Q, F])
        again(XB + 3 * CH * F * 4 + 2 * Q * TP * 4)
        upd = view([TP, CH, F])
        rest = view([TP, CH, F])
        again(XB)
        key_i = view([128, max(PW * T, TP)], i32)
        wint = view([128, BC, WIN], i32)
        iot = view([128, 128], i32)
        again(XB)
        HB = 3
        hid = view([128, HB, HS, Q * TP])
        again()
        raw = view([128, 3 * F])
        cnt = view([TP, 2, (GW + PW) * T], bf16)
        ohk = view([128, OHS, PW * T], bf16)
        ohl = view([128, OHS, 128], bf16)

        view, again = region("edge_buffers", max(3 * F * T * 2, 38400))
        dst_all = view([128, BLOCKS, BC], i32)
        src_d = view([128, DENSE, GC], i32)
        dst_d = view([128, DENSE, GC], i32)
        base_row = view([1, BLOCKS])
        pair_row = view([1, DENSE, GP])
        base_all = view([128, BLOCKS])
        b2part = view([1, 3, F], bf16)
        b2left = view([1, 2, F])
        offs = view([128, DENSE, GP])
        again()
        key_f = view([128, DENSE, GC])
        low_f = view([128, DENSE, GC])
        again()
        ea = view([2 * ED, UN, PAIRS * 128])
        zb = view([128, UN, BC, F])
        zn = view([128, 2, 2 * PAIRS, F])
        sq = view([128, 2, BC, F])
        hT = view([128, UN, PAIRS * 128])
        msg = view([128, UN, BC, F])
        again()
        hparts = view([TP, T, 3, F], bf16)

        ps = ctx.enter_context(nc.psum_tensor("ps", [128, 8, 512], f32))
        zp, tp, mp, ag = ([ps[:, 2 * k + i, :] for i in range(2)] for k in range(4))

        x_t = x.rearrange("(t p) f -> p t f", p=TP)
        out_t = out.rearrange("(t p) f -> p t f", p=TP)
        ptab_t = ptab.rearrange("(t p) f -> p t f", p=TP)
        xtab_t = xtab.rearrange("(t p) f -> p t f", p=TP)
        htab_t = htab.rearrange("(t p) f -> p t f", p=TP)

        def bcast(a, n):
            return a.unsqueeze(2).broadcast_to([a.shape[0], a.shape[1], n])

        def per_tile(a, n):
            return a.unsqueeze(1).broadcast_to([a.shape[0], n, a.shape[1]])

        NORM = 15
        def wait(eng, semaphore, value):
            if not isinstance(value, int) or value > 0:
                eng.wait_ge(semaphore, value)

        def repeated(eng, count, body, lead=1):
            for g in range(lead):
                body(g)
            with eng.Fori(lead, count) as g:
                body(g)

        turns = {}

        def wait_alone(eng, name):
            if name not in turns:
                turns[name] = sem(f"turns_of_{name}")
            eng.sem_inc(turns[name], 1)

        HALF = 6
        RSTD = 12

        def rstd_step(v, k, total, y, t):
            if k == 0:
                return v.tensor_scalar(total, total, 1.0 / F, EPS, ALU.mult, ALU.add)
            if k == 1:
                return v.tensor_scalar(t.bitcast(i32), total.bitcast(i32), 1, None, ALU.logical_shift_right)
            if k == 2:
                return v.tensor_scalar(y.bitcast(i32), t.bitcast(i32), -1.0, float(0x5F3759DF), ALU.mult, ALU.add)
            if k % 3 == 0:
                return v.scalar_tensor_tensor(t, y, -0.5, y, ALU.mult, ALU.mult)
            if k % 3 == 1:
                return v.tensor_tensor(t, t, total, ALU.mult)
            return v.scalar_tensor_tensor(y, t, 1.5, y, ALU.add, ALU.mult)

        def rstd(v, total, y, t, step, base):
            for k in range(RSTD):
                if k:
                    v.wait_ge(step, base + k)
                rstd_step(v, k, total, y, t).then_inc(step, 1)
            v.wait_ge(step, base + RSTD)

        s_zero = sem("l0_zeros_ready")
        s_fin = sem("group_keys_ready")
        s_g = sem("group_bases_broadcast")
        s_w = sem("weights_loaded")
        s_i = sem("edges_loaded")
        s_x = sem("x_loaded")
        s_iota = sem("iota_ready")
        s_const = sem("constants_ready")
        s_dstep = sem("setup_vector_steps")
        s_bp = sem("bases_broadcast")
        s_wt = sem("worst_transposed")
        s_b2 = sem("b2_split")
        s_b2l = sem("b2_rest_ready")
        s_b2r = sem("b2_repeated")
        s_cen = sem("centred")
        s_sqd = sem("squared")
        s_norm = sem("normalised")
        s_pad = sem("pad_ready")
        s_tr = sem("transposed")
        s_cp = sem("columns_copied")
        s_cT = sem("columns_in_place")
        s_pr = sem("rows_multiplied")
        s_prc = sem("rows_copied")
        s_ps = [sem(f"rows_stored{q}") for q in range(BQ)]
        s_b1 = sem("b1_repeated")
        WL = 16 * 20

        with nc.Block() as block:
            @block.sync
            def _(sp):
                sp.dma_start(w1n[F:2 * F, :], W1[0:F, :]).then_inc(s_w, 16)
                sp.dma_start(b1r[:, :], b1.unsqueeze(0)).then_inc(s_w, 16)
                sp.dma_start(wu[:, :], Wu).then_inc(s_w, 16)
                sp.dma_start(m1[:, :], M1).then_inc(s_w, 16)
                sp.dma_start(m2[:, :, :], M2.rearrange("(h p) f -> p h f", p=128)).then_inc(s_w, 16)
                for h in range(HS):
                    sp.dma_start(c1col[:, h:h + 1], c1[h * 128:(h + 1) * 128].unsqueeze(1)).then_inc(s_w, 16)
                for k in range(2):
                    sp.dma_start(gcol[k * F:(k + 1) * F, 0:1], g1.unsqueeze(1)).then_inc(s_w, 16)
                    sp.dma_start(gcol[k * F:(k + 1) * F, 1:2], be1.unsqueeze(1)).then_inc(s_w, 16)
                for k, row in enumerate((b2, bu, gn, bn, c2)):
                    sp.dma_start(rows[:, k, :], row.unsqueeze(0)).then_inc(s_w, 16)
                sp.dma_start(dst_all[:, :, :], dst).then_inc(s_i, 16)
                sp.dma_start(dst_d[:, :, :], dst_dense).then_inc(s_i, 16)
                sp.dma_start(src_all[:, :, :], src).then_inc(s_i, 16)
                sp.dma_start(src_d[:, :, :], src_dense).then_inc(s_i, 16)
                sp.wait_ge(s_const, 2)
                for k in range(2):
                    sp.dma_start(w2d[k * F:(k + 1) * F, k * F:(k + 1) * F], W2).then_inc(s_w, 16)
                    sp.dma_start(w1e[k * ED:(k + 1) * ED, k * F:(k + 1) * F], W1[F:F + ED, :]).then_inc(s_w, 16)
                sp.wait_ge(s_b2, 3)
                for k in range(3):
                    for c in range(BC):
                        sp.dma_start(b2rep[k:k + 1, c, :], b2part[:, k, :]).then_inc(s_b2r, 16)
                sp.wait_ge(s_b2r, 16 * 3 * BC)
                def chunk(g):
                    for q in range(BQ):
                        wait(sp, s_prc, BQ * g + q + 1)
                        sp.dma_start(ptab_t[:, bass.ds(g * CH + q * Q, Q), :],
                                     prow[:, q * Q:(q + 1) * Q, :]).then_inc(s_ps[q], 16)
                repeated(sp, CHUNKS, chunk)
                for q in range(BQ):
                    sp.wait_ge(s_ps[q], 16 * CHUNKS)
                sp.wait_ge(s_i, 64)

            @block.gpsimd
            def _(pool):
                def load(g):
                    wait(pool, s_x, 16 * g)
                    wait_alone(pool, "gpsimd")
                    pool.dma_start(xs[:, bass.ds(g * CH, CH), :], x_t[:, bass.ds(g * CH, CH), :]).then_inc(s_x, 16)
                load(0)
                pool.iota(iot[:, :], [[1, 128]], base=0, channel_multiplier=-1).then_inc(s_iota, 1)
                pool.iota(wint[:, :, :], [[0, BC], [1, WIN]], base=0, channel_multiplier=0).then_inc(s_iota, 1)
                pool.iota(number_i[:, :], [[0, 1]], base=0, channel_multiplier=1).then_inc(s_iota, 1)
                pool.iota(key_i[:, :], [[1, max(PW * T, TP)]], base=0, channel_multiplier=0).then_inc(s_iota, 1)
                with pool.Fori(1, CHUNKS) as g:
                    load(g)
                def chunk(g):
                    for q in range(BQ):
                        wait(pool, s_cp, BQ * g + q + 1)
                        pool.tensor_copy(cT[:, bass.ds(g * (CH * TP) + q * Q * TP, Q * TP)],
                                         cols[:, q % 2, :]).then_inc(s_cT, 1)
                repeated(pool, CHUNKS, chunk)

            @block.vector
            def _(v):
                v.memset(w2d[:, :], 0.0).then_inc(s_const, 1)
                v.memset(w1e[:, :], 0.0).then_inc(s_const, 1)
                v.memset(ones_b[:, :], 1.0).then_inc(s_const, 1)
                v.memset(ones[:, :], 1.0).then_inc(s_const, 1)
                v.memset(hpad[:, :, 0:F], 0.0).then_inc(s_const, 1)
                v.memset(cT[:, N:N + GW], 0.0).then_inc(s_const, 1)
                v.wait_ge(s_iota, 4)
                v.tensor_scalar(ident[:, :], iot[:, :], 0.0, None, ALU.is_equal).then_inc(s_const, 1)
                v.tensor_copy(winf[:, :, :], wint[:, :, :]).then_inc(s_const, 1)
                v.tensor_copy(keyf[:, :], key_i[:, 0:PW * T]).then_inc(s_const, 1)
                v.tensor_copy(lowf[:, :], key_i[:, 0:TP]).then_inc(s_const, 1)
                def chunk(g):
                    wait(v, s_x, 16 * g + 16)
                    wait_alone(v, "vector")
                    xg = xs[:, bass.ds(g * CH, CH), :]
                    v.tensor_reduce(stat[:, 0, :], xg, X, ALU.add).then_inc(s_norm, 1)
                    wait(v, s_norm, NORM * g + 1)
                    v.tensor_scalar(stat[:, 1, :], stat[:, 0, :], 1.0 / F, None, ALU.mult).then_inc(s_norm, 1)
                    wait(v, s_norm, NORM * g + 2)
                    wait(v, s_pad, g)
                    v.tensor_tensor(xc[:, :, :], xg, bcast(stat[:, 1, :], F), ALU.subtract).then_inc(s_cen, 1)
                    wait(v, s_sqd, g + 1)
                    v.tensor_reduce(stat[:, 2, :], sqc[:, :, :], X, ALU.add).then_inc(s_norm, 1)
                    wait(v, s_norm, NORM * g + 3)
                    rstd(v, stat[:, 2, :], stat[:, 3, :], stat[:, 0, :], s_norm, NORM * g + 3)
                    wait(v, s_cen, 2 * g + 1)
                    v.tensor_tensor(xc[:, :, :], xc[:, :, :], bcast(stat[:, 3, :], F), ALU.mult).then_inc(s_cen, 1)
                chunk(0)
                v.wait_ge(s_w, WL)
                for k, (lo, w) in enumerate(((F, w1n[F:2 * F, :]), (0, w1e[0:ED, 0:F]), (ED, w1e[ED:2 * ED, F:2 * F]),
                                             (0, b1r[:, :]))):
                    m = wmean[lo:lo + w.shape[0], k:k + 1]
                    v.tensor_reduce(m, w, X, ALU.add).then_inc(s_dstep, 1)
                    v.wait_ge(s_dstep, 3 * k + 1)
                    v.tensor_scalar(m, m, 1.0 / F, None, ALU.mult).then_inc(s_dstep, 1)
                    v.wait_ge(s_dstep, 3 * k + 2)
                    v.tensor_scalar(w, w, m, None, ALU.subtract).then_inc(s_dstep, 1)
                v.tensor_copy(b2part[:, 0, :], rows[:, 0, :]).then_inc(s_b2, 1)
                for k in range(2):
                    v.wait_ge(s_b2, k + 1)
                    if k:
                        v.wait_ge(s_b2l, k)
                    v.tensor_tensor(b2left[:, k, :], b2left[:, 0, :] if k else rows[:, 0, :], b2part[:, k, :],
                                    ALU.subtract).then_inc(s_b2l, 1)
                    v.wait_ge(s_b2l, k + 1)
                    v.tensor_copy(b2part[:, k + 1, :], b2left[:, k, :]).then_inc(s_b2, 1)
                v.wait_ge(s_dstep, 12)
                v.tensor_copy(b1q[:, :, :], per_tile(b1r[:, :], Q)).then_inc(s_b1, 1)
                with v.Fori(1, CHUNKS) as g:
                    chunk(g)
                v.wait_ge(s_i, 64)
                v.tensor_copy(base_int[:, :], dst_all[0:1, :, 0]).then_inc(s_dstep, 1)
                v.tensor_copy(base_row[:, :], dst_all[0:1, :, 0]).then_inc(s_dstep, 1)
                v.tensor_copy(pair_row[:, :, :], dst_d[0:1, :, 0:GC:2]).then_inc(s_dstep, 1)
                for k in range(BANKS):
                    lo, n = 512 * k, min(512, BLOCKS - 512 * k)
                    v.wait_ge(s_bp, k + 1)
                    v.tensor_copy(base_all[:, lo:lo + n], ag[k][:, 0:n]).then_inc(s_dstep, 1)
                v.wait_ge(s_dstep, 15 + BANKS)
                v.tensor_tensor(rel_all[:, :, :], dst_all[:, :, :], bcast(base_all[:, :], BC),
                                ALU.subtract).then_inc(s_dstep, 1)
                v.wait_ge(s_dstep, 16 + BANKS)
                for k in range(GBANKS):
                    lo, hi = k * PER, min((k + 1) * PER, DENSE)
                    v.wait_ge(s_g, k + 1)
                    first = zp[k][:, 0:(hi - lo) * GP].rearrange("p (s q) -> p s q", q=GP)
                    v.tensor_tensor(key_f[:, lo:hi, 0:GC:2], dst_d[:, lo:hi, 0:GC:2], first,
                                    ALU.subtract).then_inc(s_dstep, 1)
                    v.tensor_tensor(key_f[:, lo:hi, 1:GC:2], dst_d[:, lo:hi, 1:GC:2], first[:, :, 0:GC // 2],
                                    ALU.subtract).then_inc(s_dstep, 1)
                    v.tensor_tensor(offs[:, lo:hi, :], first,
                                    bcast(base_all[:, (G0 + lo) * UN:(G0 + hi) * UN:UN], GP),
                                    ALU.subtract).then_inc(s_dstep, 1)
                nb = 16 + BANKS + 3 * GBANKS
                v.wait_ge(s_dstep, nb)
                gaps = dst_d[:, :, 0:GP - 1].bitcast(f32)
                v.tensor_tensor(gaps, offs[:, :, 1:GP], offs[:, :, 0:GP - 1], ALU.subtract).then_inc(s_dstep, 1)
                v.wait_ge(s_dstep, nb + 1)
                tests = ((rel_all[:, :, :], ALU.max, 1.0, 1.0 - WIN), (rel_all[:, :, :], ALU.min, -1.0, 0.0),
                         (key_f[:, :, :], ALU.max, 1.0, 1.0 - PW), (key_f[:, :, :], ALU.min, -1.0, 0.0),
                         (offs[:, :, :], ALU.max, 1.0, float(PW - GW)), (gaps, ALU.max, 1.0, 1.0 - PW))
                for k, (t, op, _, _) in enumerate(tests):
                    v.tensor_reduce(worst[:, k:k + 1], t, XY, op).then_inc(s_dstep, 1)
                v.wait_ge(s_dstep, nb + 7)
                for k, (_, _, by, plus) in enumerate(tests):
                    v.tensor_scalar(worst[:, k:k + 1], worst[:, k:k + 1], by, plus, ALU.mult, ALU.add).then_inc(s_dstep, 1)
                v.wait_ge(s_dstep, nb + 13)
                v.tensor_reduce(worst[:, 6:7], worst[:, 0:6], X, ALU.max).then_inc(s_dstep, 1)
                v.tensor_scalar(low_f[:, :, :], src_d[:, :, :], 1.0 / TP, -(TP - 1) / 2 / TP,
                                ALU.mult, ALU.add).then_inc(s_dstep, 1)
                v.wait_ge(s_dstep, nb + 15)
                v.tensor_scalar(low_f[:, :, :], low_f[:, :, :], float(3 << 22), float(3 << 22),
                                ALU.add, ALU.subtract).then_inc(s_dstep, 1)
                v.wait_ge(s_dstep, nb + 16)
                v.scalar_tensor_tensor(key_f[:, :, :], key_f[:, :, :], float(T), low_f[:, :, :],
                                       ALU.mult, ALU.add).then_inc(s_dstep, 1)
                v.wait_ge(s_dstep, nb + 17)
                v.scalar_tensor_tensor(low_f[:, :, :], low_f[:, :, :], float(-TP), src_d[:, :, :],
                                       ALU.mult, ALU.add).then_inc(s_dstep, 1)
                v.wait_ge(s_dstep, nb + 18)
                v.tensor_copy(keys_all[:, 0:DENSE, 0:GC], key_f[:, :, :]).then_inc(s_fin, 1)
                v.tensor_copy(keys_all[:, 0:DENSE, GC:2 * GC], low_f[:, :, :]).then_inc(s_fin, 1)
                v.memset(keys_all[:, DENSE, :], 0.0).then_inc(s_fin, 1)
                v.tensor_scalar(at_int[:, :, :], offs[0:1, :, :], float(T), None, ALU.mult).then_inc(s_dstep, 1)
                v.tensor_copy(number[:, :], number_i[:, :]).then_inc(s_dstep, 1)
                v.wait_ge(s_dstep, nb + 20)
                v.wait_ge(s_wt, 1)
                v.tensor_scalar(held_all[:, :], offs[:, :, GP - 1], number[:, 0:1], float(PW),
                                ALU.subtract, ALU.add).then_inc(s_dstep, 1)
                v.wait_ge(s_dstep, nb + 21)
                v.tensor_scalar(held_all[:, :], held_all[:, :], 0.0, None, ALU.is_gt).then_inc(s_dstep, 1)
                v.tensor_reduce(worst_row[:, :], ag[0][0:1, 0:128], X, ALU.max).then_inc(s_dstep, 1)
                v.wait_ge(s_dstep, nb + 23)
                v.tensor_scalar(flag[:, :], worst_row[:, :], 0.0, None, ALU.is_gt).then_inc(s_dstep, 1)
                v.wait_ge(s_bp, BANKS + 1)
                v.tensor_copy(gb[:, :, :], ag[1][:, 0:3 * F].rearrange("p (k f) -> p k f", k=3)).then_inc(s_dstep, 1)

            @block.scalar
            def _(a):
                def square(g):
                    wait(a, s_cen, 2 * g + 1)
                    a.activation(sqc[:, :, :], xc[:, :, :], ACT.Square).then_inc(s_sqd, 1)

                def relu(g):
                    wait(a, s_cen, 2 * g + 2)
                    wait(a, s_tr, BQ * g)
                    a.activation(hpad[:, :, F:2 * F], xc[:, :, :], ACT.Relu).then_inc(s_pad, 1)

                def columns(g, q):
                    wait(a, s_tr, BQ * g + q + 1)
                    wait(a, s_cT, BQ * g + max(q - 1, 0))
                    wait(a, s_pr, BQ * g + max(q - 1, 0))
                    a.activation(cols[:, q % 2, :], tp[q % 2][:, 0:Q * TP], ACT.Copy).then_inc(s_cp, 1)

                def table_rows(g, q):
                    wait(a, s_pr, BQ * g + q + 1)
                    wait(a, s_ps[q], 16 * g)
                    a.activation(prow[:, q * Q:(q + 1) * Q, :],
                                 mp[q % 2][0:TP, 0:Q * F].rearrange("p (t f) -> p t f", t=Q),
                                 ACT.Copy).then_inc(s_prc, 1)

                def step(g):
                    last = g - 1
                    for q in range(BQ):
                        if q == min(2, BQ - 1) and not (isinstance(g, int) and g == CHUNKS):
                            square(g)
                        if not isinstance(g, int) or g > 0:
                            columns(last, q)
                            if q:
                                table_rows(last, q - 1)
                    if not isinstance(g, int) or g > 0:
                        table_rows(last, BQ - 1)
                    if not (isinstance(g, int) and g == CHUNKS):
                        relu(g)
                a.wait_ge(s_const, 10)
                repeated(a, CHUNKS, step, 2)
                step(CHUNKS)

            @block.tensor
            def _(pe):
                pe.wait_ge(s_const, 10)
                pe.wait_ge(s_dstep, 12)
                pe.wait_ge(s_b1, 1)
                def turn(g, q):
                    wait(pe, s_cp, BQ * g + max(q - 1, 0))
                    wait_alone(pe, "tensor")
                    for t in range(Q):
                        mm = pe.transpose(tp[q % 2][:, t * TP:(t + 1) * TP], hpad[:, q * Q + t, :],
                                          ident[0:TP, 0:TP])
                    mm.then_inc(s_tr, 1)

                def chunk(g):
                    wait(pe, s_pad, g + 1)
                    turn(g, 0)
                    for q in range(BQ):
                        if q < BQ - 1:
                            turn(g, q + 1)
                        wait(pe, s_cp, BQ * g + q + 1)
                        wait(pe, s_prc, BQ * g + max(q - 1, 0))
                        pe.matmul(mp[q % 2][0:TP, 0:Q * F], ones[:, 0:TP], b1q[:, :, :].rearrange("o t f -> o (t f)"),
                                  start=True, stop=False)
                        for t in range(Q):
                            mm = pe.matmul(mp[q % 2][0:TP, t * F:(t + 1) * F], cols[F:2 * F, q % 2, t * TP:(t + 1) * TP],
                                           w1n[F:2 * F, :], start=False, stop=(t == Q - 1))
                        mm.then_inc(s_pr, 1)
                repeated(pe, CHUNKS - 1, chunk)
                pe.wait_ge(s_dstep, 15)
                for k in range(BANKS):
                    lo, n = 512 * k, min(512, BLOCKS - 512 * k)
                    pe.matmul(ag[k][:, 0:n], ones[:, :], base_row[:, lo:lo + n], start=True, stop=True).then_inc(s_bp, 1)
                for k in range(GBANKS):
                    lo, hi = k * PER, min((k + 1) * PER, DENSE)
                    pe.matmul(zp[k][:, 0:(hi - lo) * GP], ones[:, :],
                              pair_row[:, lo:hi, :].rearrange("o s q -> o (s q)"), start=True, stop=True).then_inc(s_g, 1)
                chunk(CHUNKS - 1)
                pe.wait_ge(s_dstep, 15 + BANKS)
                pe.matmul(ag[1][:, 0:3 * F], ones[:, :], rows[:, 2:5, :].rearrange("o k f -> o (k f)"),
                          start=True, stop=True).then_inc(s_bp, 1)
                pe.wait_ge(s_dstep, 16 + BANKS + 3 * GBANKS + 14)
                pe.transpose(ag[0][0:1, 0:128], worst[:, 6:7], ident[:, :]).then_inc(s_wt, 1)

        def gather(pool, table, n, j, done):
            for c in range(BC):
                pool.indirect_dma_start(
                    out=gat[:, j, c, :], out_offset=None, in_=table[:, :],
                    in_offset=bass.IndirectOffsetOnAxis(ap=idx[:, j, c:c + 1], axis=0)).then_inc(done, 16)

        def edge_products(pe, j):
            for k in range(PAIRS):
                two = 2 * k + 1 < BC
                mm = pe.matmul(zp[j % 2][:, 2 * k * F:(2 * k + 1 + two) * F],
                               ea[0:(1 + two) * ED, j, k * 128:(k + 1) * 128],
                               w1e[0:(1 + two) * ED, 0:(1 + two) * F], start=True, stop=True)
            return mm

        def transposes(pe, j):
            for k in range(PAIRS):
                mm = pe.transpose(tp[j % 2][:, k * 128:(k + 1) * 128],
                                  zn[:, j % 2, 2 * k:2 * k + 2, :].rearrange("p c f -> p (c f)"), ident[:, :])
            return mm

        def second_products(pe, j):
            o = mp[j % 2]
            pe.matmul(o[:, 0:BC * F], ones_b[:, :], b2rep[:, :, :].rearrange("o c f -> o (c f)"),
                      start=True, stop=False, skip_group_check=True)
            for k in range(BC // 2):
                mm = pe.matmul(o[:, k * 128:(k + 1) * 128], hT[:, j, k * 128:(k + 1) * 128], w2d[:, :],
                               start=False, stop=(k == PAIRS - 1), skip_group_check=True)
            if BC % 2:
                k = BC // 2
                mm = pe.matmul(o[:, k * 128:k * 128 + F], hT[0:F, j, k * 128:(k + 1) * 128],
                               w2d[0:F, 0:F], start=False, stop=True, skip_group_check=True)
            return mm

        def window_sums(pe, j, rows_of, to=ag):
            for c in range(BC):
                mm = pe.matmul(to[j % 2][0:F, 0:WIN], rows_of[:, c, :], oh[:, j, c, :],
                               start=(c == 0), stop=(c == BC - 1))
            return mm

        def one_hot(v, j, rel):
            return v.tensor_tensor(oh[:, j, :, :], winf[:, :, :], bcast(rel, WIN), ALU.is_equal)

        def block_of(t, n):
            return t[:, n, :] if isinstance(n, int) else t[:, bass.ds(n, 1), :].rearrange("p o c -> p (o c)")

        def load_edges(sp, n, j, done):
            def of(t):
                return t[n, :, :] if isinstance(n, int) else t[bass.ds(n, 1), :, :].rearrange("o k e -> (o k) e")
            sp.dma_start(ea[:, j, 0:(BC // 2) * 128], of(edge_pairs)).then_inc(done, 16)
            sp.dma_start(ea[0:ED, j, (BC // 2) * 128:], of(edge_last)).then_inc(done, 16)

        def indices(a, n, j):
            return a.activation(idx[:, j, :], block_of(src_all, n), ACT.Copy)

        def add_sums(v, n, j, of=ag):
            b = v.value_load(base_int[0:1, bass.ds(n, 1)], min_val=0, max_val=N)
            to = cT[0:F, bass.ds(b, WIN)]
            return v.tensor_tensor(to, to, of[j % 2][0:F, 0:WIN], ALU.add)

        def before(j):
            return 1 if j == 0 else 2

        def lagged(r, j, lag):
            r2, j2 = r + (j - lag) // UN, (j - lag) % UN
            return r2, j2, r2 * UN + j2

        def there(n):
            return not isinstance(n, int) or 0 <= n < BLOCKS

        def rounds(eng, step, lag, lead=1):
            for j in range(lead * UN):
                step(j // UN, j % UN)
            with eng.Fori(lead, ROUNDS - 1) as r:
                for j in range(UN):
                    step(r, j)
            for j in range(UN + lag):
                step(ROUNDS - 1, j)

        def flagged(eng):
            return eng.value_load(flag[0:1, 0:1], min_val=0, max_val=1)

        g_idx = sem("l0_index_ready")
        g_ea = [sem(f"l0_edges_loaded{j}") for j in range(UN)]
        g_gat = [sem(f"l0_rows_gathered{j}") for j in range(UN)]
        g_ep = sem("l0_edge_products")
        g_z = sem("l0_z_ready")
        g_sq = sem("l0_z_squared")
        g_red = sem("l0_squares_summed")
        g_ra = sem("l0_rstd_first_steps")
        g_rb = sem("l0_rstd_last_steps")
        g_n = sem("l0_z_normalised")
        g_t = sem("l0_z_transposed")
        g_h = sem("l0_hidden_ready")
        g_m = sem("l0_second_products")
        g_msg = sem("l0_messages_ready")
        g_oh = sem("l0_one_hot_ready")
        g_sum = sem("l0_window_summed")
        g_add = sem("l0_sums_added")

        with nc.Block() as block:
            @block.sync
            def _(sp):
                def step(r, j):
                    n = r * UN + j
                    wait(sp, g_ep, n - UN + 1)
                    load_edges(sp, n, j, g_ea[j])
                with sp.If(flagged(sp) == 0):
                    rounds(sp, step, 0)

            @block.gpsimd
            def _(pool):
                def step(r, j):
                    n = r * UN + j
                    wait(pool, g_idx, n + 1)
                    wait(pool, g_z, n - UN + 1)
                    wait_alone(pool, "gpsimd")
                    gather(pool, ptab, n, j, g_gat[j])
                with pool.If(flagged(pool) == 0):
                    rounds(pool, step, 0)

            @block.tensor
            def _(pe):
                def step(r, j):
                    _, s, n = lagged(r, j, 3)
                    if there(n):
                        wait(pe, g_n, n + 1)
                        wait(pe, g_h, n + 1 - before(s))
                        transposes(pe, s).then_inc(g_t, 1)
                    _, s, n = lagged(r, j, 4)
                    if there(n):
                        wait(pe, g_h, n + 1)
                        wait(pe, g_msg, n + 1 - before(s))
                        second_products(pe, s).then_inc(g_m, 1)
                    q, s, n = lagged(r, j, -1)
                    if there(n):
                        wait(pe, g_ea[s], q * 32 + 32)
                        wait(pe, g_z, n + 1 - before(s))
                        edge_products(pe, s).then_inc(g_ep, 1)
                    _, s, n = lagged(r, j, 5)
                    if there(n):
                        wait(pe, g_msg, n + 1)
                        wait(pe, g_oh, n + 1)
                        wait(pe, g_add, n + 1 - before(s))
                        window_sums(pe, s, msg[:, s, :, :]).then_inc(g_sum, 1)
                pe.wait_ge(s_zero, 1)
                with pe.If(flagged(pe) == 0):
                    pe.wait_ge(g_ea[0], 32)
                    edge_products(pe, 0).then_inc(g_ep, 1)
                    rounds(pe, step, 5, lead=2)

            @block.scalar
            def _(a):
                def step(r, j):
                    _, s, n = lagged(r, j, 0)
                    if there(n):
                        wait(a, g_z, n + 1)
                        wait(a, g_red, n + 1 - before(s))
                        a.activation(sq[:, s % 2, :, :], zb[:, s, :, :], ACT.Square).then_inc(g_sq, 1)
                        if there(n + UN):
                            indices(a, n + UN, s).then_inc(g_idx, 1)
                    _, s, n = lagged(r, j, 3)
                    if there(n):
                        wait(a, g_t, n + 1)
                        wait(a, g_m, n + 1 - UN)
                        a.activation(hT[:, s, :], tp[s % 2][:, 0:PAIRS * 128], ACT.Silu,
                                     bias=gcol[:, 1:2], scale=gcol[:, 0:1]).then_inc(g_h, 1)
                    _, s, n = lagged(r, j, 4)
                    if there(n):
                        wait(a, g_m, n + 1)
                        wait(a, g_sum, n + 1 - UN)
                        a.activation(msg[:, s, :, :], mp[s % 2][:, 0:BC * F].rearrange("p (c f) -> p c f", c=BC),
                                     ACT.Silu).then_inc(g_msg, 1)
                with a.If(flagged(a) == 0):
                    for j in range(UN):
                        indices(a, j, j).then_inc(g_idx, 1)
                    rounds(a, step, 4, lead=2)

            @block.vector
            def _(v):
                def first_step(k, s, n):
                    if there(n):
                        wait(v, g_ra if k else g_red, n * HALF + k if k else n + 1)
                        rstd_step(v, k, st[:, s, 0, :], st[:, s, 1, :], st[:, s, 2, :]).then_inc(g_ra, 1)

                def last_step(k, s, n):
                    if there(n):
                        wait(v, g_rb if k else g_ra, n * HALF + (k if k else HALF))
                        rstd_step(v, HALF + k, st[:, s, 0, :], st[:, s, 1, :], st[:, s, 2, :]).then_inc(g_rb, 1)

                def step(r, j):
                    q, s, n = lagged(r, j, 0)
                    _, s1, n1 = lagged(r, j, 1)
                    _, s2, n2 = lagged(r, j, 2)
                    _, s3, n3 = lagged(r, j, 3)
                    _, s6, n6 = lagged(r, j, 6)
                    last_step(0, s2, n2)
                    first_step(0, s1, n1)
                    if there(n):
                        wait(v, g_ep, n + 1)
                        wait(v, g_gat[s], q * (16 * BC) + 16 * BC)
                        wait(v, g_n, n + 1 - UN)
                        v.tensor_tensor(zb[:, s, :, :], zp[s % 2][:, 0:BC * F].rearrange("p (c f) -> p c f", c=BC),
                                        gat[:, s, :, :], ALU.add).then_inc(g_z, 1)
                    last_step(1, s2, n2)
                    first_step(1, s1, n1)
                    if there(n3):
                        wait(v, g_sum, n3 + 1 - UN)
                        one_hot(v, s3, block_of(rel_all, n3)).then_inc(g_oh, 1)
                    last_step(2, s2, n2)
                    first_step(2, s1, n1)
                    if there(n6):
                        wait(v, g_sum, n6 + 1)
                        wait(v, g_add, n6)
                        add_sums(v, n6, s6).then_inc(g_add, 1)
                    last_step(3, s2, n2)
                    first_step(3, s1, n1)
                    if there(n):
                        wait(v, g_sq, n + 1)
                        v.tensor_reduce(st[:, s, 0, :], sq[:, s % 2, :, :], X, ALU.add).then_inc(g_red, 1)
                    for k in range(4, HALF):
                        last_step(k, s2, n2)
                        first_step(k, s1, n1)
                    if there(n2):
                        wait(v, g_rb, n2 * HALF + HALF)
                        wait(v, g_t, n2 + 1 - before(s2))
                        v.tensor_tensor(zn[:, s2 % 2, 0:BC, :], zb[:, s2, :, :], bcast(st[:, s2, 1, :], F),
                                        ALU.mult).then_inc(g_n, 1)
                v.memset(zn[:, :, :, :], 0.0).then_inc(s_zero, 1)
                v.wait_ge(s_zero, 1)
                with v.If(flagged(v) == 0):
                    rounds(v, step, 6, lead=2)

        def general(layer, table):
            def gsem(name):
                return sem(f"general{layer}_{name}")
            x_done, x_idx, x_ea, x_gat, x_ep = map(gsem, ("block_done", "index_ready", "edges_loaded", "rows_gathered", "edge_products"))
            x_z, x_sq, x_st, x_n, x_t = map(gsem, ("z_ready", "squared", "rstd_steps", "normalised", "transposed"))
            x_h, x_m, x_msg, x_rel, x_oh = map(gsem, ("hidden_ready", "second_products", "messages_ready", "window_steps", "one_hot_ready"))
            x_sum, x_add = map(gsem, ("window_summed", "sums_added"))

            x_dst = gsem("dst_loaded")

            def sync(sp):
                with sp.Fori(0, BLOCKS) as n:
                    sp.wait_ge(x_done, n + 1)
                    sp.dma_start(dst_n[:, :], block_of(dst, n)).then_inc(x_dst, 16)
                    if layer == 0:
                        load_edges(sp, n, 0, x_ea)

            def gpsimd(pool):
                with pool.Fori(0, BLOCKS) as n:
                    pool.wait_ge(x_idx, n + 1)
                    wait_alone(pool, "gpsimd")
                    gather(pool, table, n, 0, x_gat)

            def scalar(a):
                with a.Fori(0, BLOCKS) as n:
                    a.wait_ge(x_done, n + 1)
                    indices(a, n, 0).then_inc(x_idx, 1)
                    if layer == 0:
                        a.wait_ge(x_z, n + 1)
                        a.activation(sq[:, 0, :, :], gat[:, 0, :, :], ACT.Square).then_inc(x_sq, 1)
                        a.wait_ge(x_t, n + 1)
                        a.activation(hT[:, 0, :], tp[0][:, 0:PAIRS * 128], ACT.Silu,
                                     bias=gcol[:, 1:2], scale=gcol[:, 0:1]).then_inc(x_h, 1)
                        a.wait_ge(x_m, n + 1)
                        a.activation(msg[:, 0, :, :], mp[0][:, 0:BC * F].rearrange("p (c f) -> p c f", c=BC),
                                     ACT.Silu).then_inc(x_msg, 1)

            def tensor(pe):
                with pe.Fori(0, BLOCKS) as n:
                    if layer == 0:
                        pe.wait_ge(x_ea, 32 * n + 32)
                        pe.wait_ge(x_done, n + 1)
                        edge_products(pe, 0).then_inc(x_ep, 1)
                        pe.wait_ge(x_n, n + 1)
                        transposes(pe, 0).then_inc(x_t, 1)
                        pe.wait_ge(x_h, n + 1)
                        second_products(pe, 0).then_inc(x_m, 1)
                        pe.wait_ge(x_msg, n + 1)
                    else:
                        pe.wait_ge(x_gat, n * (16 * BC) + 16 * BC)
                    wait_alone(pe, "tensor")
                    with pe.Fori(0, WINDOWS) as w:
                        k = n * WINDOWS + w
                        pe.wait_ge(x_oh, k + 1)
                        pe.wait_ge(x_add, k + 1)
                        window_sums(pe, 0, msg[:, 0, :, :] if layer == 0 else gat[:, 0, :, :]).then_inc(x_sum, 1)

            def vector(v):
                v.sem_inc(x_done, 1)
                v.sem_inc(x_sum, 1)
                v.sem_inc(x_add, 1)
                with v.Fori(0, BLOCKS) as n:
                    v.wait_ge(x_dst, 16 * n + 16)
                    v.memset(wbase[:, :], 0.0).then_inc(x_rel, 1)
                    if layer == 0:
                        v.wait_ge(x_ep, n + 1)
                        v.wait_ge(x_gat, n * (16 * BC) + 16 * BC)
                        z = gat[:, 0, :, :]
                        v.tensor_tensor(z, zp[0][:, 0:BC * F].rearrange("p (c f) -> p c f", c=BC), z,
                                        ALU.add).then_inc(x_z, 1)
                        v.wait_ge(x_sq, n + 1)
                        v.tensor_reduce(st[:, 0, 0, :], sq[:, 0, :, :], X, ALU.add).then_inc(x_st, 1)
                        v.wait_ge(x_st, n * (RSTD + 1) + 1)
                        rstd(v, st[:, 0, 0, :], st[:, 0, 1, :], st[:, 0, 2, :], x_st, n * (RSTD + 1) + 1)
                        v.tensor_tensor(zn[:, 0, 0:BC, :], z, bcast(st[:, 0, 1, :], F), ALU.mult).then_inc(x_n, 1)
                    with v.Fori(0, WINDOWS) as w:
                        k = n * WINDOWS + w
                        v.wait_ge(x_rel, k * 2 + n + 1)
                        v.tensor_scalar(reln[:, :], dst_n[:, :], wbase[:, :], None, ALU.subtract).then_inc(x_rel, 1)
                        v.wait_ge(x_rel, k * 2 + n + 2)
                        v.wait_ge(x_sum, k + 1)
                        one_hot(v, 0, reln[:, :]).then_inc(x_oh, 1)
                        v.tensor_scalar(wbase[:, :], wbase[:, :], float(WIN), None, ALU.add).then_inc(x_rel, 1)
                        v.wait_ge(x_sum, k + 2)
                        v.wait_ge(x_add, k + 1)
                        to = cT[0:F, bass.ds(w * WIN, WIN)]
                        v.tensor_tensor(to, to, ag[0][0:F, 0:WIN], ALU.add).then_inc(x_add, 1)
                    v.wait_ge(x_add, n * WINDOWS + WINDOWS + 1)
                    v.wait_ge(x_oh, n * WINDOWS + WINDOWS)
                    v.sem_inc(x_done, 1)

            with nc.Block() as block:
                @block.sync
                def _(sp):
                    with sp.If(flagged(sp) != 0):
                        sync(sp)

                @block.gpsimd
                def _(pool):
                    with pool.If(flagged(pool) != 0):
                        gpsimd(pool)

                @block.tensor
                def _(pe):
                    with pe.If(flagged(pe) != 0):
                        tensor(pe)

                @block.scalar
                def _(a):
                    with a.If(flagged(a) != 0):
                        scalar(a)

                @block.vector
                def _(v):
                    with v.If(flagged(v) != 0):
                        vector(v)

        general(0, ptab)

        u_w = sem("update_columns_ready")
        u_u = sem("update_products")
        u_s = sem("update_ready")
        u_v = sem("update_vector_steps")
        u_c = sem("update_centred")
        u_q = sem("update_squared")
        u_h = sem("layer1_h_ready")
        u_hi = sem("h_high_part")
        u_left = sem("h_rest")
        u_mid = sem("h_middle_part")
        u_low = sem("h_low_part")
        u_x = sem("residual_steps")
        u_st = sem("layer1_rows_stored")
        u_xst = sem("residual_stored")
        u_t = sem("layer1_transposed")
        u_cp = sem("layer1_columns_copied")

        def parts_of(g):
            return hparts[:, bass.ds(g * CH, CH), :, :]

        with nc.Block() as block:
            @block.gpsimd
            def _(pool):
                def low_part(g):
                    wait(pool, u_left, g + 1)
                    wait(pool, u_mid, g + 1)
                    pool.tensor_tensor(parts_of(g)[:, :, 2, :], rest[:, :, :], parts_of(g)[:, :, 1, :],
                                       ALU.subtract).then_inc(u_low, 1)

                def chunk(g):
                    for q in range(BQ):
                        wait(pool, u_u, BQ * g + max(q - 1, 0))
                        pool.tensor_copy(cols[:, q % 2, :],
                                         cT[:, bass.ds(g * (CH * TP) + q * Q * TP, Q * TP)]).then_inc(u_w, 1)
                    if not isinstance(g, int) or g > 1:
                        low_part(g - 2)
                repeated(pool, CHUNKS, chunk, 2)
                low_part(CHUNKS - 2)
                low_part(CHUNKS - 1)

            @block.tensor
            def _(pe):
                def update(g):
                    for q in range(BQ):
                        wait(pe, u_w, BQ * g + q + 1)
                        wait(pe, u_s, BQ * g + max(q - 1, 0))
                        for t in range(Q):
                            o = mp[q % 2][0:TP, t * F:(t + 1) * F]
                            pe.matmul(o, ones[:, 0:TP], rows[:, 1, :], start=True, stop=False)
                            mm = pe.matmul(o, cols[:, q % 2, t * TP:(t + 1) * TP], wu[:, :],
                                           start=False, stop=True)
                        mm.then_inc(u_u, 1)

                def turn_rows(g):
                    wait(pe, u_h, g + 1)
                    for q in range(BQ):
                        wait(pe, u_cp, BQ * g + max(q - 1, 0))
                        wait_alone(pe, "tensor")
                        for t in range(Q):
                            mm = pe.transpose(tp[q % 2][0:F, t * TP:(t + 1) * TP], prow[:, q * Q + t, :],
                                              ident[0:TP, 0:TP])
                        mm.then_inc(u_t, 1)

                def step(g):
                    update(g)
                    if not isinstance(g, int) or g > 0:
                        turn_rows(g - 1)
                repeated(pe, CHUNKS, step, 2)
                turn_rows(CHUNKS - 1)

            @block.scalar
            def _(a):
                def silu(g):
                    for q in range(BQ):
                        wait(a, u_u, BQ * g + q + 1)
                        wait(a, u_c, 2 * g - 1)
                        a.activation(upd[:, q * Q:(q + 1) * Q, :],
                                     mp[q % 2][0:TP, 0:Q * F].rearrange("p (t f) -> p t f", t=Q),
                                     ACT.Silu).then_inc(u_s, 1)

                def square(g, k):
                    wait(a, u_c, 2 * g + k + 1)
                    a.activation(sqc[:, :, :], xc[:, :, :], ACT.Square).then_inc(u_q, 1)

                def table_rows(g):
                    wait(a, u_v, g * (2 * NORM + 2) + 2 * NORM + 2)
                    wait(a, u_st, 16 * g)
                    wait(a, u_t, BQ * g)
                    wait(a, u_left, g)
                    a.activation(prow[:, :, :], xc[:, :, :], ACT.Relu).then_inc(u_h, 1)
                    wait(a, u_h, g + 1)
                    a.activation(parts_of(g)[:, :, 0, :], prow[:, :, :], ACT.Copy).then_inc(u_hi, 1)
                    for q in range(BQ):
                        wait(a, u_t, BQ * g + q + 1)
                        a.activation(cT[0:F, bass.ds(g * (CH * TP) + q * Q * TP, Q * TP)],
                                     tp[q % 2][0:F, 0:Q * TP], ACT.Copy).then_inc(u_cp, 1)

                def middle_part(g):
                    wait(a, u_left, g + 1)
                    a.activation(parts_of(g)[:, :, 1, :], rest[:, :, :], ACT.Copy).then_inc(u_mid, 1)

                def step(g):
                    if not isinstance(g, int) or g > 0:
                        square(g - 1, 0)
                    silu(g)
                    if not isinstance(g, int) or g > 1:
                        middle_part(g - 2)
                    if not isinstance(g, int) or g > 0:
                        square(g - 1, 1)
                        table_rows(g - 1)
                repeated(a, CHUNKS, step, 2)
                square(CHUNKS - 1, 0)
                middle_part(CHUNKS - 2)
                square(CHUNKS - 1, 1)
                table_rows(CHUNKS - 1)
                middle_part(CHUNKS - 1)

            @block.vector
            def _(v):
                def mean_of(of, base):
                    v.tensor_reduce(stat[:, 0, :], of, X, ALU.add).then_inc(u_v, 1)
                    v.wait_ge(u_v, base + 1)
                    v.tensor_scalar(stat[:, 1, :], stat[:, 0, :], 1.0 / F, None, ALU.mult).then_inc(u_v, 1)
                    v.wait_ge(u_v, base + 2)

                def scale(base, g, k):
                    v.wait_ge(u_q, 2 * g + k + 1)
                    v.tensor_reduce(stat[:, 2, :], sqc[:, :, :], X, ALU.add).then_inc(u_v, 1)
                    v.wait_ge(u_v, base + 3)
                    rstd(v, stat[:, 2, :], stat[:, 3, :], stat[:, 0, :], u_v, base + 3)
                    v.wait_ge(u_c, 2 * g + k + 1)
                    v.tensor_tensor(xc[:, :, :], xc[:, :, :], bcast(stat[:, 3, :], F), ALU.mult).then_inc(u_v, 1)

                def without_high(g):
                    wait(v, u_hi, g + 1)
                    wait(v, u_mid, g)
                    wait(v, u_low, g)
                    v.tensor_tensor(rest[:, :, :], prow[:, :, :], parts_of(g)[:, :, 0, :], ALU.subtract).then_inc(u_left, 1)

                def chunk(g):
                    first, second = g * (2 * NORM + 2), g * (2 * NORM + 2) + NORM + 1
                    xg = xs[:, bass.ds(g * CH, CH), :]
                    wait(v, u_s, BQ * g + BQ)
                    mean_of(upd[:, :, :], first)
                    wait(v, u_h, g)
                    v.tensor_tensor(xc[:, :, :], upd[:, :, :], bcast(stat[:, 1, :], F), ALU.subtract).then_inc(u_c, 1)
                    if not isinstance(g, int) or g > 0:
                        without_high(g - 1)
                    scale(first, g, 0)
                    wait(v, u_v, second)
                    v.tensor_tensor(xc[:, :, :], xc[:, :, :], per_tile(gb[0:TP, 0, :], CH), ALU.mult).then_inc(u_x, 1)
                    wait(v, u_x, 3 * g + 1)
                    v.tensor_tensor(xc[:, :, :], xc[:, :, :], per_tile(gb[0:TP, 1, :], CH), ALU.add).then_inc(u_x, 1)
                    wait(v, u_x, 3 * g + 2)
                    v.tensor_tensor(xg, xg, xc[:, :, :], ALU.add).then_inc(u_x, 1)
                    wait(v, u_x, 3 * g + 3)
                    wait_alone(v, "vector")
                    mean_of(xg, second)
                    v.tensor_tensor(xc[:, :, :], xg, bcast(stat[:, 1, :], F), ALU.subtract).then_inc(u_c, 1)
                    scale(second, g, 1)
                repeated(v, CHUNKS, chunk, 2)
                without_high(CHUNKS - 1)

            @block.sync
            def _(sp):
                def chunk(g):
                    wait(sp, u_x, 3 * g + 3)
                    sp.dma_start(xtab_t[:, bass.ds(g * CH, CH), :], xs[:, bass.ds(g * CH, CH), :]).then_inc(u_xst, 16)
                    wait(sp, u_h, g + 1)
                    sp.dma_start(htab_t[:, bass.ds(g * CH, CH), :], prow[:, :, :]).then_inc(u_st, 16)
                repeated(sp, CHUNKS, chunk)
                sp.wait_ge(u_st, 16 * CHUNKS)
                sp.wait_ge(u_xst, 16 * CHUNKS)

        k_idx = sem("l1_index_ready")
        k_gat = [sem(f"l1_rows_gathered{j}") for j in range(UN)]
        k_oh = sem("l1_one_hot_ready")
        k_sum = sem("l1_window_summed")
        k_add = sem("l1_sums_added")
        d_zero = sem("counts_zeroed")
        d_load = sem("group_keys_loaded")
        d_half = sem("column_keys_compared")
        d_key = sem("column_one_hots_ready")
        d_use = sem("columns_multiplied")
        d_first = sem("pair_first_node_added")
        d_copy = sem("pair_nodes_copied")
        d_sum = sem("group_summed")
        d_raw = sem("group_sums_copied")
        d_turn = sem("group_sums_turned")
        d_add = sem("group_sums_added")
        WT = PW // 3 * T
        built = [ps[:TP, 3 * k:3 * k + 3, 0:WT] for k in range(2)]
        wide = ps[:, 6, 0:3 * F]
        turned = ps[0:F, 7, 128:128 + GW]
        agl = [ps[:, 7, :]] * 2

        PARTS = 12

        def two(body):
            def both(e):
                body(2 * e, 0)
                body(2 * e + 1, 1)
            return both

        def columns_back(c):
            return OHS if c >= OHS else c + GC - max(k for k in range(GC) if k % OHS == c)

        def group_of(t, d):
            return t[:, d, :] if isinstance(d, int) else t[:, bass.ds(d, 1), :].rearrange("p o c -> p (o c)")

        with nc.Block() as block:
            @block.gpsimd
            def _(pool):
                def step(r, j):
                    n = r * UN + j
                    wait(pool, k_idx, n + 1)
                    wait(pool, k_sum, n - UN + 1)
                    wait_alone(pool, "gpsimd")
                    gather(pool, htab, n, j, k_gat[j])

                def both(r):
                    for j in range(UN):
                        step(r, j)
                with pool.If(flagged(pool) == 0):
                    repeated(pool, G0, both)

            @block.scalar
            def _(a):
                def index(r, j):
                    n = r * UN + j
                    wait(a, k_sum, n - UN + 1)
                    indices(a, n, j).then_inc(k_idx, 1)

                def raw_sums(d):
                    wait(a, d_sum, d + 1)
                    wait(a, d_turn, d)
                    held = held_all[:, d:d + 1] if isinstance(d, int) else held_all[:, bass.ds(d, 1)]
                    a.activation(raw[:, :], wide, ACT.Copy, scale=held).then_inc(d_raw, 1)

                def both(d, s):
                    for q in range(GP):
                        at = a.value_load(group_of(at_int, d)[:, q:q + 1], min_val=0, max_val=GW * T)
                        wait(a, d_use, d * GC + min(2 * q + 2, GC))
                        if q == 0:
                            wait(a, d_sum, d - 1)
                        pair = built[(s * GP + q) % 2]
                        wait(a, d_copy, (d * GP + q) * 2)
                        a.activation(cnt[:, s, bass.ds(at + WT, 2 * WT)].rearrange("p (b k) -> p b k", b=2),
                                     pair[:, 1:3, :], ACT.Copy).then_inc(d_copy, 1)
                        wait(a, d_first, d * GP + q + 1)
                        a.activation(cnt[:, s, bass.ds(at + T, WT - T)], pair[:, 0, T:WT], ACT.Copy).then_inc(d_copy, 1)
                        if q % 2 == 1 and q < 2 * UN:
                            index(d + 1, q // 2)
                    if not (isinstance(d, int) and d == 0):
                        raw_sums(d - 1)
                with a.If(flagged(a) == 0):
                    for j in range(UN):
                        index(0, j)
                    a.wait_ge(d_zero, 1)
                    repeated(a, DENSE // 2, two(both))
                    raw_sums(DENSE - 1)

            @block.tensor
            def _(pe):
                def sums(r, j):
                    n = r * UN + j
                    wait(pe, k_gat[j], r * (16 * BC) + 16 * BC)
                    wait(pe, k_oh, n + 1)
                    wait(pe, k_add, n)
                    if j == 0:
                        wait(pe, d_add, r - 1)
                    window_sums(pe, j, gat[:, j, :, :], agl).then_inc(k_sum, 1)

                def product(d, s, lo, hi):
                    if lo == 0:
                        wait(pe, d_first, d * GP + GP)
                        wait(pe, d_copy, (d * GP + GP) * 2)
                        wait(pe, d_raw, d)
                    for t in range(lo, hi):
                        mm = pe.matmul(wide, cnt[:, s, t:t + (GW - 1) * T + 1:T],
                                       hparts[:, t, :, :].rearrange("p k f -> p (k f)"), start=(t == 0), stop=(t == T - 1))
                    if hi == T:
                        mm.then_inc(d_sum, 1)

                def turn(d):
                    wait(pe, d_raw, d + 1)
                    wait(pe, k_add, (d + 2) * UN)
                    wait(pe, d_add, d)
                    for k in range(3):
                        mm = pe.matmul(turned, raw[:, k * F:(k + 1) * F], ident[:, :], start=(k == 0), stop=(k == 2))
                    mm.then_inc(d_turn, 1)

                def both(d, s):
                    for q in range(GP):
                        wait(pe, d_first, d * GP + q - 1)
                        wait(pe, d_copy, (d * GP + q - 1) * 2)
                        for c in range(2 * q, min(2 * q + 2, GC)):
                            wait(pe, d_key, d * GC + c + 1)
                            for b in range(3):
                                mm = pe.matmul(built[(s * GP + q) % 2][:, b, :], ohl[:, c % OHS, 0:TP],
                                               ohk[:, c % OHS, b * WT:(b + 1) * WT],
                                               start=(c == 2 * q), stop=(c == min(2 * q + 1, GC - 1)))
                            mm.then_inc(d_use, 1)
                        if q % 2 == 1 and q < 2 * UN:
                            sums(d, q // 2)
                        if q == 0 and not (isinstance(d, int) and d < 2):
                            turn(d - 2)
                        if not (isinstance(d, int) and d == 0):
                            if 1 <= q <= PARTS:
                                product(d - 1, 1 - s, (q - 1) * T // PARTS, q * T // PARTS)
                with pe.If(flagged(pe) == 0):
                    repeated(pe, DENSE // 2, two(both))
                    product(DENSE - 1, 1, 0, T)
                    turn(DENSE - 2)
                    for j in range(UN):
                        sums(DENSE, j)
                    turn(DENSE - 1)

            @block.vector
            def _(v):
                def one_hots(r, j):
                    n = r * UN + j
                    wait(v, k_sum, n + 1 - UN)
                    one_hot(v, j, block_of(rel_all, n)).then_inc(k_oh, 1)

                def add_block(r, j):
                    n = r * UN + j
                    wait(v, k_sum, n + 1)
                    wait(v, k_add, n)
                    wait(v, d_add, r - 1)
                    add_sums(v, n, j, agl).then_inc(k_add, 1)

                def add_group(d):
                    base = v.value_load(base_int[0:1, bass.ds((d + G0) * UN, 1)], min_val=0, max_val=N)
                    wait(v, d_turn, d + 1)
                    wait(v, k_add, (d + 2) * UN)
                    wait(v, d_add, d)
                    to = cT[0:F, bass.ds(base, GW)]
                    v.tensor_tensor(to, to, turned, ALU.add).then_inc(d_add, 1)

                def add_first(d, s, q):
                    y = d * GP + q
                    if q == 0:
                        wait(v, d_use, d * GC + 2)
                        wait(v, d_sum, d - 1)
                        v.tensor_copy(cnt[:, s, 0:T], built[s * GP % 2][:, 0, 0:T]).then_inc(d_first, 1)
                        return
                    at = v.value_load(group_of(at_int, d)[:, q:q + 1], min_val=0, max_val=GW * T)
                    wait(v, d_use, d * GC + min(2 * q + 2, GC))
                    wait(v, d_copy, y * 2)
                    wait(v, d_first, y)
                    to = cnt[:, s, bass.ds(at, T)]
                    v.tensor_tensor(to, to, built[(s * GP + q) % 2][:, 0, 0:T], ALU.add).then_inc(d_first, 1)

                def load_keys(d):
                    wait_alone(v, "vector")
                    v.tensor_copy(keys[:, :], group_of(keys_all, d)).then_inc(d_load, 1)

                def both(d, s):
                    wait(v, d_load, d + 1)
                    for c in range(GC):
                        wait(v, d_use, d * GC + c + 1 - columns_back(c))
                        v.tensor_scalar(ohk[:, c % OHS, :], keyf[:, :], keys[:, c:c + 1], None, ALU.is_equal)\
                         .then_inc(d_half, 1)
                        v.tensor_scalar(ohl[:, c % OHS, 0:TP], lowf[:, :], keys[:, GC + c:GC + c + 1], None, ALU.is_equal)\
                         .then_inc(d_key, 1)
                        if c % 2 == 1 and c > 1:
                            add_first(d, s, c // 2 - 1)
                        if c == 1 and not (isinstance(d, int) and d == 0):
                            add_first(d - 1, 1 - s, GP - 1)
                        if c == 4 and not (isinstance(d, int) and d < 2):
                            add_group(d - 2)
                        if c % 4 == 2 and c // 4 < UN - 1:
                            one_hots(d, c // 4 + 1)
                        if c % 4 == 2 and c >= 6:
                            add_block(d, c // 4 - 1)
                    wait(v, d_key, d * GC + GC)
                    load_keys(d + 1)
                    add_first(d, s, GP - 2)
                    one_hots(d + 1, 0)
                with v.If(flagged(v) == 0):
                    v.memset(cnt[:, :, :], 0.0).then_inc(d_zero, 1)
                    v.wait_ge(s_fin, 3)
                    load_keys(0)
                    v.wait_ge(d_zero, 1)
                    one_hots(0, 0)
                    repeated(v, DENSE // 2, two(both))
                    add_first(DENSE - 1, 1, GP - 1)
                    add_group(DENSE - 2)
                    for j in range(UN):
                        if j:
                            one_hots(DENSE, j)
                        add_block(DENSE, j)
                    add_group(DENSE - 1)

        general(1, htab)

        e_h = sem("mlp_hidden_products")
        e_r = sem("mlp_hidden_ready")
        e_o = sem("mlp_products")
        e_ld = [sem(f"residual_loaded{q}") for q in range(BQ)]
        e_c = sem("mlp_bias_added")
        e_x = sem("result_ready")
        e_st = sem("result_stored")
        hp = [[ps[:, HS * k + h, 0:Q * TP] for h in range(HS)] for k in range(HB)]
        op = [ps[0:TP, HS * HB + k, 0:Q * F] for k in range(2)]
        BATCHES = T // Q
        assert HS * HB + 2 <= 8

        def slot_back(q, slots):
            return slots if q >= slots else q + BQ - max(k for k in range(BQ) if k % slots == q)

        def batches(g):
            return [(q, g * BQ + q) for q in range(BQ)]

        with nc.Block() as block:
            @block.gpsimd
            def _(pool):
                def chunk(g):
                    for q, b in batches(g):
                        wait(pool, e_c, b + 1 - BQ)
                        pool.dma_start(xs[:, bass.ds(b * Q, Q), :], xtab_t[:, bass.ds(b * Q, Q), :]).then_inc(e_ld[q], 16)
                repeated(pool, CHUNKS, chunk)

            @block.tensor
            def _(pe):
                def second(q, b):
                    wait(pe, e_r, HS * b + HS)
                    wait(pe, e_x, b + 1 - slot_back(q, 2))
                    for t in range(Q):
                        for h in range(HS):
                            mm = pe.matmul(op[q % 2][:, t * F:(t + 1) * F], hid[:, q % HB, h, t * TP:(t + 1) * TP],
                                           m2[:, h, :], start=(h == 0), stop=(h == HS - 1))
                    mm.then_inc(e_o, 1)

                def chunk(g):
                    for q, b in batches(g):
                        wait(pe, e_r, HS * (b + 1 - slot_back(q, HB)))
                        for h in range(HS):
                            pe.matmul(hp[q % HB][h], m1[:, h * 128:(h + 1) * 128],
                                      cT[0:F, bass.ds(b * (Q * TP), Q * TP)], start=True, stop=True).then_inc(e_h, 1)
                        if not (isinstance(b, int) and b == 0):
                            second((q - 1) % BQ, b - 1)
                repeated(pe, CHUNKS, chunk)
                second(BQ - 1, BATCHES - 1)

            @block.scalar
            def _(a):
                def chunk(g):
                    for q, b in batches(g):
                        wait(a, e_o, b + 1 - slot_back(q, HB))
                        for h in range(HS):
                            wait(a, e_h, HS * b + h + 1)
                            a.activation(hid[:, q % HB, h, :], hp[q % HB][h], ACT.Relu,
                                         bias=c1col[:, h:h + 1]).then_inc(e_r, 1)
                repeated(a, CHUNKS, chunk)

            @block.vector
            def _(v):
                def chunk(g):
                    for q, b in batches(g):
                        xb = xs[:, bass.ds(b * Q, Q), :]
                        wait(v, e_ld[q], g * 16 + 16)
                        v.tensor_tensor(xb, xb, per_tile(gb[0:TP, 2, :], Q), ALU.add).then_inc(e_c, 1)
                        wait(v, e_c, b + 1)
                        wait(v, e_o, b + 1)
                        v.tensor_tensor(xb, xb, op[q % 2].rearrange("p (t f) -> p t f", t=Q), ALU.add).then_inc(e_x, 1)
                repeated(v, CHUNKS, chunk)

            @block.sync
            def _(sp):
                def chunk(g):
                    for q, b in batches(g):
                        wait(sp, e_x, b + 1)
                        sp.dma_start(out_t[:, bass.ds(b * Q, Q), :], xs[:, bass.ds(b * Q, Q), :]).then_inc(e_st, 16)
                repeated(sp, CHUNKS, chunk)
                sp.wait_ge(e_st, 16 * BATCHES)


BLOCK_COLUMNS = 5
INPUTS = ["x", "src", "dst", "src_dense", "dst_dense", "edge_pairs", "edge_last", "L0_gnn_W1", "L0_gnn_b1", "L0_gnn_g1", "L0_gnn_be1", "L0_gnn_W2", "L0_gnn_b2",
          "L0_gnn_Wu", "L0_gnn_bu", "L0_gnn_gn", "L0_gnn_bn", "L1_gnn_W1", "L1_gnn_b1", "L1_gnn_W2", "L1_gnn_b2"]


def kernel(x, src, dst, edge_attr_32, **weights):
    import numpy as np
    import concourse.bacc as bacc
    from concourse.bass_utils import run_bass_kernel_spmd

    E, ED = edge_attr_32.shape
    edges = 128 * BLOCK_COLUMNS
    blocks = E // edges
    rounds, columns = blocks // 5, 5 * BLOCK_COLUMNS
    arrays = {"x": np.ascontiguousarray(x)}
    for name, a in (("src", src), ("dst", dst)):
        arrays[name] = np.ascontiguousarray(np.asarray(a).reshape(blocks, 128, BLOCK_COLUMNS).transpose(1, 0, 2))
        arrays[name + "_dense"] = np.ascontiguousarray(
            np.asarray(a).reshape(rounds, columns, 128)[(rounds + 1) // 2:].transpose(2, 0, 1))
    ea = np.asarray(edge_attr_32).reshape(blocks, 128, BLOCK_COLUMNS, ED)
    pairs = BLOCK_COLUMNS // 2
    arrays["edge_pairs"] = np.ascontiguousarray(
        ea[:, :, :2 * pairs].reshape(blocks, 128, pairs, 2, ED).transpose(0, 3, 4, 2, 1)
        .reshape(blocks, 2 * ED, pairs * 128))
    arrays["edge_last"] = np.ascontiguousarray(ea[:, :, 2 * pairs].transpose(0, 2, 1))
    for name, a in weights.items():
        arrays[name] = np.ascontiguousarray(a)

    nc = bacc.Bacc("TRN2", target_bir_lowering=False, num_devices=1)
    args = [nc.dram_tensor(f"in_{n}", arrays[n].shape, mybir.dt.from_np(arrays[n].dtype), kind="ExternalInput").ap()
            for n in INPUTS]
    out = nc.dram_tensor("out", arrays["x"].shape, mybir.dt.float32, kind="ExternalOutput").ap()
    build_gnn(nc, *args, out)
    r = run_bass_kernel_spmd(nc, [{f"in_{n}": arrays[n] for n in INPUTS}], core_ids=[0])
    return r.results[0]["out"]
```
